# Optimizing a Trainium2 kernel written in Bass

```python
import numpy as np
import jax
import jax.numpy as jnp

def _softmax(x, axis=-1):
    return jax.nn.softmax(x, axis=axis)

def _gelu(x):
    return jax.nn.gelu(x, approximate=True)

def _silu(x):
    return jax.nn.silu(x)

def _sigmoid(x):
    return jax.nn.sigmoid(x)

def _layernorm(x, axis=-1, eps=1e-05):
    m = jnp.mean(x, axis=axis, keepdims=True)
    v = jnp.var(x, axis=axis, keepdims=True)
    return (x - m) / jnp.sqrt(v + eps)

def _scatter_add(tgt, idx, src, axis=0):
    return tgt.at[idx].add(src)

def _segment_sum(src, seg, n):
    return jax.ops.segment_sum(src, seg, n)
kernel_name = 'mk_gnn_preln_d1_gnn_r8_51b739'

def setup_inputs(seed: int=0):
    np.random.seed(seed)
    _w = jnp.asarray

    def _rec_inputs():
        import jax
        import jax.numpy as jnp
        _gk = jax.random.key(seed)
        x = -0.0003713 + 1 * jax.random.normal(jax.random.fold_in(_gk, 1), (12500, 128), jnp.float32)
        src = jax.random.randint(jax.random.fold_in(_gk, 2), (200000,), 0, 12500, jnp.int32)
        dst = jax.random.randint(jax.random.fold_in(_gk, 3), (200000,), 0, 12500, jnp.int32)
        _o = jnp.argsort(dst, stable=True)
        src = src[_o]
        dst = dst[_o]
        edge_type_3 = jax.random.randint(jax.random.fold_in(_gk, 12), (200000,), 0, 3, jnp.int32)
        edge_weight = jax.random.uniform(jax.random.fold_in(_gk, 13), (200000,), jnp.float32, 0.0, 0.999999)
        return (x, src, dst, edge_type_3, edge_weight)
    x, src, dst, edge_type_3, edge_weight = _rec_inputs()

    def _L0_gnn_setup():
        import jax, jax.numpy as jnp
        import numpy as np
        N_NODES = 12500
        N_EDGES = 75000
        D = 128
        N_TYPES = 3
        key = jax.random.key(seed)
        ks = jax.random.split(key, 10)
        x = jax.random.normal(ks[0], (N_NODES, D), dtype=jnp.float32)
        edge_index = jax.random.randint(ks[1], (2, N_EDGES), 0, N_NODES, dtype=jnp.int64)
        edge_type_ids = jax.random.randint(ks[2], (N_EDGES,), 0, N_TYPES, dtype=jnp.int32)
        edge_weights = jax.random.uniform(ks[3], (N_EDGES,), dtype=jnp.float32)
        limit = float(np.sqrt(6.0 / (D + D)))
        W_edge = jax.random.uniform(ks[4], (N_TYPES, D, D), minval=-limit, maxval=limit, dtype=jnp.float32)
        b_edge = jnp.zeros((N_TYPES, D), dtype=jnp.float32)
        W_self = jax.random.uniform(ks[5], (D, D), minval=-limit, maxval=limit, dtype=jnp.float32)
        b_self = jnp.zeros((D,), dtype=jnp.float32)
        attention = jnp.ones((N_TYPES + 1,), dtype=jnp.float32) / (N_TYPES + 1)
        return {'x': x, 'edge_index': edge_index, 'edge_type_ids': edge_type_ids, 'edge_weights': edge_weights, 'W_edge': W_edge, 'b_edge': b_edge, 'W_self': W_self, 'b_self': b_self, 'attention': attention}
    _L0_gnn_all = _L0_gnn_setup()
    _L0_gnn_in = {k: v for k, v in _L0_gnn_all.items() if k in ('W_edge', 'b_edge', 'W_self', 'b_self', 'attention')}
    del _L0_gnn_all
    return {'x': x, 'src': src, 'dst': dst, 'edge_type_3': edge_type_3, 'edge_weight': edge_weight, 'L0_gnn_W_edge': _L0_gnn_in['W_edge'], 'L0_gnn_b_edge': _L0_gnn_in['b_edge'], 'L0_gnn_W_self': _L0_gnn_in['W_self'], 'L0_gnn_b_self': _L0_gnn_in['b_self'], 'L0_gnn_attention': _L0_gnn_in['attention']}

def reference(x, src, dst, edge_type_3, edge_weight, L0_gnn_W_edge, L0_gnn_b_edge, L0_gnn_W_self, L0_gnn_b_self, L0_gnn_attention):
    import jax
    import jax.numpy as jnp

    def _L0_gnn_ref(x, edge_index, edge_type_ids, edge_weights, W_edge, b_edge, W_self, b_self, attention):
        import jax, jax.numpy as jnp
        import numpy as np
        N_NODES = 12500
        N_EDGES = 75000
        D = 128
        N_TYPES = 3
        n_nodes = x.shape[0]
        n_types = W_edge.shape[0]
        src, dst = (edge_index[0], edge_index[1])
        xs = x[src]
        outs = []
        for t in range(n_types):
            m = jnp.where(edge_type_ids == t, edge_weights, jnp.zeros((), x.dtype))
            y = (xs @ W_edge[t] + b_edge[t]) * m[:, None]
            outs.append(jax.ops.segment_sum(y, dst, num_segments=n_nodes))
        outs.append(x @ W_self + b_self)
        stacked = jnp.stack(outs, axis=-1)
        attn = jax.nn.softmax(attention)
        out = jnp.sum(stacked * attn, axis=-1)
        return jax.nn.gelu(out, approximate=False)
    edge_index = jnp.stack([src, dst])
    h = jnp.maximum(_layernorm(x, axis=-1), 0.0)
    x = x + _L0_gnn_ref(h, edge_index, edge_type_3, edge_weight, L0_gnn_W_edge, L0_gnn_b_edge, L0_gnn_W_self, L0_gnn_b_self, L0_gnn_attention)
    return x

_drawn_inputs = setup_inputs


def setup_inputs(seed=0):
    import zlib

    import numpy as np

    out = dict(_drawn_inputs(seed))
    spreads = {'L0_gnn_b_edge': (0.0, 0.1), 'L0_gnn_b_self': (0.0, 0.59), 'L0_gnn_attention': (0.25, 0.6)}
    factors = {}
    for name, (base, spread) in spreads.items():
        noise = np.random.default_rng([zlib.crc32(name.encode()), seed]).standard_normal(out[name].shape)
        drawn = base * np.exp(spread * noise) if base else spread * noise
        out[name] = jnp.asarray(drawn.astype(out[name].dtype))
    for name, factor in factors.items():
        out[name] = (out[name] * factor).astype(out[name].dtype)
    return out
```

```python
import concourse.bass as bass
from concourse import mybir
from contextlib import ExitStack


def gnn_layer(nc, x, src, dst, edge_type, edge_weight, w_edge, b_edge, w_self, b_self, attention, out):
    fp32 = mybir.dt.float32
    i32 = mybir.dt.int32
    ALU = mybir.AluOpType
    ACT = mybir.ActivationFunctionType
    AX = mybir.AxisListType
    ds = bass.ds

    P = 128
    NODES, D = x.shape
    EDGES = src.shape[0]
    TYPES = w_edge.shape[0]
    TPG = 4
    GE = TPG * P
    GROUPS = -(-EDGES // GE)
    LAST_EDGES = EDGES - (GROUPS - 1) * GE
    LAST_TILES = -(-LAST_EDGES // P)
    RING = 3
    ITERS = (GROUPS - 1) // RING
    assert ITERS * RING == GROUPS - 1
    WIN = 42
    SW = TYPES * WIN
    BLOCKS = -(-NODES // P)
    LAST_ROWS = NODES - (BLOCKS - 1) * P
    COLS = BLOCKS * P
    assert NODES + WIN <= COLS and BLOCKS < ITERS
    EPS = 1e-5
    ROWC = -(-GROUPS // P)
    ROWS = [min(P, GROUPS - c * P) for c in range(ROWC)]
    SELF = TPG
    OUTB = 7
    OSTEPS = BLOCKS // OUTB
    assert OSTEPS * OUTB == BLOCKS and OSTEPS % 2 == 0
    SPLIT = 4

    ctx = ExitStack()
    with ctx:
        def sb(name, shape, dt=fp32):
            return ctx.enter_context(nc.sbuf_tensor(name, shape, dt))

        def sem(name):
            return ctx.enter_context(nc.semaphore(name))

        acc = sb("acc", [P, COLS])
        xres = sb("xres", [P, BLOCKS * D])
        src_row = sb("src_row", [P, ROWC, GE], i32)
        dst_row = sb("dst_row", [P, ROWC, GE], i32)
        typ_row = sb("typ_row", [P, ROWC, GE], i32)
        ew_row = sb("ew_row", [P, ROWC, GE])
        srcf_row = sb("srcf_row", [P, GE])
        rel_row = sb("rel_row", [P, GE])
        side_row = sb("side_row", [P, GE])
        typ1_row = sb("typ1_row", [P, GE])
        key_row = sb("key_row", [P, GE])
        first_dst = sb("first_dst", [P, 4])
        base_col = sb("base_col", [P, 2])
        shift = sb("shift", [P, 1])
        src_all = sb("src_all", [P, GROUPS * TPG])
        meta_all = sb("meta_all", [P, GROUPS * 2 * TPG])
        base_row = sb("base_row", [1, GROUPS], i32)
        span_row = sb("span_row", [1, GROUPS])
        span_max = sb("span_max", [1, 1], i32)
        idx = sb("idx", [P, RING, TPG], i32)
        meta = sb("meta", [P, RING, 2 * TPG])
        raw = sb("raw", [P, RING, TPG * D])
        stats = sb("stats", [P, RING, TPG + 1, 6])
        meanvar = sb("meanvar", [P, RING, TPG + 1, 2])
        negmean = sb("negmean", [P, RING, TPG + 1])
        std = sb("std", [P, RING, TPG + 1])
        rstd = sb("rstd", [P, RING, TPG + 1])
        scale = sb("scale", [P, RING, TPG])
        hid = sb("hid", [P, RING, TPG, D])
        select = sb("select", [P, RING, TPG, SW])
        sums = sb("sums", [P, RING, SW])
        wsum = sb("wsum", [P, RING, WIN])
        hid_self = sb("hid_self", [P, D])
        diag = sb("diag", [P, P])
        hidT_self = sb("hidT_self", [P, P])
        gel = sb("gel", [P, 2, OUTB * P])
        ident = sb("ident", [P, P])
        iota_i = sb("iota_i", [P, SW], i32)
        iota = sb("iota", [P, SW])
        fold = sb("fold", [P, WIN])
        zeros = sb("zeros", [P, COLS // 16])
        eps = sb("eps", [P, 1])
        wts = sb("wts", [P, TYPES, D])
        wself = sb("wself", [P, D])
        brep = sb("brep", [P, D])
        bself = sb("bself", [P, 1])
        att = sb("att", [P, TYPES + 1])
        att_col = sb("att_col", [P, 1])
        att_max = sb("att_max", [P, 2])
        att_sum = sb("att_sum", [P, 2])

        def bank(name):
            return ctx.enter_context(nc.psum_tensor(name, [P, 512], fp32))

        agg = [bank(f"agg{i}") for i in range(RING)]
        co = [bank(f"co{i}") for i in range(RING)]
        selfT = bank("selfT")
        selfO = bank("selfO")
        OUT0 = 64

        consts_ready = sem("consts_ready")
        pool_step = sem("pool_step")
        att_loaded = sem("att_loaded")
        wts_loaded = sem("wts_loaded")
        acc_zeroed = sem("acc_zeroed")
        x_loaded = sem("x_loaded")
        prep_step = sem("prep_step")
        exp_done = sem("exp_done")
        max_done = sem("max_done")
        acc_final = sem("acc_final")
        settled = sem("settled")
        weights_ready = sem("weights_ready")
        span_ready = sem("span_ready")
        src_loaded = [sem(f"src_loaded{c}") for c in range(ROWC)]
        row_loaded = [sem(f"row_loaded{c}") for c in range(ROWC)]
        srcf_ready = sem("srcf_ready")
        srcT_done = sem("srcT_done")
        srcT_copied = sem("srcT_copied")
        row_step = sem("row_step")
        key_step = sem("key_step")
        key_ready = sem("key_ready")
        keyT_done = sem("keyT_done")
        keyT_copied = sem("keyT_copied")
        slot_free = sem("slot_free")
        gathered = [sem(f"gathered{u}") for u in range(RING)]
        meta_ready = sem("meta_ready")
        bn_done = sem("bn_done")
        aggr_done = sem("aggr_done")
        stats_ready = sem("stats_ready")
        std_ready = sem("std_ready")
        rstd_done = sem("rstd_done")
        scale_done = sem("scale_done")
        hid_ready = sem("hid_ready")
        select_ready = sem("select_ready")
        summed = sem("summed")
        sums_ready = sem("sums_ready")
        wsum_ready = sem("wsum_ready")
        weighted = sem("weighted")
        acc_added = sem("acc_added")
        selfT_done = sem("selfT_done")
        selfT_ready = sem("selfT_ready")
        self_done = sem("self_done")
        self_added = sem("self_added")
        gel_ready = sem("gel_ready")
        gelT_done = sem("gelT_done")
        out_ready = sem("out_ready")
        out_stored = sem("out_stored")

        SRC_DMAS = [1] * (ROWC - 1) + [3]
        ROW_DMAS = [3] * (ROWC - 1) + [8]
        GATHER_INC = [16 * TPG * ITERS + (16 * LAST_TILES if u == 0 else 0) for u in range(RING)]

        def settle(eng):
            eng.sem_inc(settled, 1)

        def tiles(g):
            return LAST_TILES if isinstance(g, int) and g == GROUPS - 1 else TPG

        def there(g):
            return not isinstance(g, int) or 0 <= g < GROUPS

        def late(g):
            return not isinstance(g, int) or g >= RING

        def walk(eng, step):
            for g in range(2 * RING):
                step(g // RING, g % RING, g, True)
            with eng.Fori(2, BLOCKS) as it:
                g0 = eng.snap(it * RING)
                for u in range(RING):
                    step(it, u, g0 + u, True)
            with eng.Fori(BLOCKS, ITERS - 1) as it:
                g0 = eng.snap(it * RING)
                for u in range(RING):
                    step(it, u, g0 + u, False)
            for g in range((ITERS - 1) * RING, GROUPS + RING):
                step(g // RING, g % RING, g, False)

        def passes(eng, body):
            limit = eng.alloc_register("pass_limit")
            eng.reg_mov(limit, 1)
            with eng.Fori(0, limit) as p:
                body(p)
                eng.wait_ge(span_ready, p + 1)
                settle(eng)
                eng.load(limit, span_max[0:1, 0:1])
                eng.reg_div(limit, limit, WIN)
                eng.reg_add(limit, limit, 1)

        block = ctx.enter_context(nc.Block())

        @block.sync
        def _(sp):
            def one_pass(p):
                for c in range(ROWC - 1):
                    lo, hi = c * P * GE, (c + 1) * P * GE
                    sp.dma_start(src_row[:, c, :], src[lo:hi].rearrange("(p e) -> p e", p=P)).then_inc(src_loaded[c], 16)
                    sp.dma_start(dst_row[:, c, :], dst[lo:hi].rearrange("(p e) -> p e", p=P)).then_inc(row_loaded[c], 16)
                    sp.dma_start(typ_row[:, c, :], edge_type[lo:hi].rearrange("(p e) -> p e", p=P)).then_inc(row_loaded[c], 16)
                    sp.dma_start(ew_row[:, c, :], edge_weight[lo:hi].rearrange("(p e) -> p e", p=P)).then_inc(row_loaded[c], 16)
                c, n = ROWC - 1, ROWS[-1] - 1
                lo, hi = c * P * GE, (GROUPS - 1) * GE
                fill = GE - LAST_EDGES
                sp.wait_ge(consts_ready, 1)
                for a, rows, signal in ((src, src_row, src_loaded[c]), (dst, dst_row, row_loaded[c]),
                                        (edge_type, typ_row, row_loaded[c]), (edge_weight, ew_row, row_loaded[c])):
                    sp.dma_start(rows[0:n, c, :], a[lo:hi].rearrange("(p e) -> p e", p=n)).then_inc(signal, 16)
                    sp.dma_start(rows[n:n + 1, c, 0:LAST_EDGES], a[hi:EDGES].rearrange("(p e) -> p e", p=1)).then_inc(signal, 16)
                    if a is not edge_weight:
                        sp.dma_start(rows[n:n + 1, c, LAST_EDGES:GE], a[EDGES - fill:EDGES].rearrange("(p e) -> p e", p=1)).then_inc(signal, 16)
                with sp.If(p < 1):
                    sp.dma_start(acc[:, :].rearrange("p (r c) -> p r c", r=16),
                                 zeros[:, :].unsqueeze(1).to_broadcast([P, 16, COLS // 16])).then_inc(acc_zeroed, 16)
                    sp.dma_start(xres[:, 0:D], x[0:P, :]).then_inc(x_loaded, 16)
                    with sp.Fori(1, BLOCKS - 1) as b:
                        sp.wait_ge(x_loaded, b * 16)
                        sp.dma_start(xres[:, ds(b * D, D)], x[ds(b * P, P), :]).then_inc(x_loaded, 16)
                    sp.wait_ge(x_loaded, (BLOCKS - 1) * 16)
                    sp.dma_start(xres[0:LAST_ROWS, (BLOCKS - 1) * D:], x[(BLOCKS - 1) * P:, :]).then_inc(x_loaded, 16)
                sp.wait_ge(acc_added, (p + 1) * GROUPS)

            passes(sp, one_pass)

            with sp.Fori(0, OSTEPS - 1) as o:
                sp.wait_ge(out_ready, o + 1)
                sp.dma_start(out[ds(o * (OUTB * P), OUTB * P), :].rearrange("(b p) d -> p b d", p=P),
                             xres[:, ds(o * (OUTB * D), OUTB * D)].rearrange("p (b d) -> p b d", d=D)).then_inc(out_stored, 16)
            sp.wait_ge(out_ready, OSTEPS)
            b0 = (OSTEPS - 1) * OUTB
            sp.dma_start(out[b0 * P:(BLOCKS - 1) * P, :].rearrange("(b p) d -> p b d", p=P),
                         xres[:, b0 * D:(BLOCKS - 1) * D].rearrange("p (b d) -> p b d", d=D)).then_inc(out_stored, 16)
            sp.dma_start(out[(BLOCKS - 1) * P:, :], xres[0:LAST_ROWS, (BLOCKS - 1) * D:]).then_inc(out_stored, 16)
            sp.wait_ge(out_stored, 16 * (OSTEPS + 1))

        @block.gpsimd
        def _(pool):
            nc.gpsimd.memset(ew_row[:, ROWC - 1, :], 0.0)
            nc.gpsimd.memset(xres[:, (BLOCKS - 1) * D:], 0.0)
            nc.gpsimd.memset(zeros[:, :], 0.0)
            nc.gpsimd.memset(eps[:, :], EPS)
            nc.gpsimd.memset(shift[:, :], 0.0)
            nc.gpsimd.iota(iota_i[:, :], pattern=[[1, SW]], base=1, channel_multiplier=0)
            nc.gpsimd.memset(ident[:, :], 0.0)
            nc.gpsimd.memset(fold[:, :], 0.0).then_inc(pool_step, 1)
            pool.wait_ge(pool_step, 1)
            nc.gpsimd.affine_select(out=ident[:, :], in_=ident[:, :], compare_op=ALU.not_equal, fill=1.0,
                                    base=0, pattern=[[-1, P]], channel_multiplier=1)
            nc.gpsimd.tensor_copy(iota[:, :], iota_i[:, :])
            for t in range(TYPES):
                nc.gpsimd.affine_select(out=fold[:, :], in_=fold[:, :], compare_op=ALU.not_equal, fill=1.0,
                                        base=-t * WIN, pattern=[[-1, WIN]], channel_multiplier=1).then_inc(pool_step, 1)
                pool.wait_ge(pool_step, 2 + t)
            nc.gpsimd.drain().then_inc(consts_ready, 1)

            def one_pass(p):
                def step(it, u, g, with_block):
                    if not there(g):
                        return
                    pool.wait_ge(slot_free, p * GROUPS + g + 1)
                    settle(pool)
                    for j in range(tiles(g)):
                        nc.gpsimd.indirect_dma_start(
                            raw[:, u, j * D:(j + 1) * D], None, x[:, :],
                            bass.IndirectOffsetOnAxis(ap=idx[:, u, j:j + 1], axis=0)).then_inc(gathered[u], 16)

                walk(pool, step)

            passes(pool, one_pass)

        @block.scalar
        def _(act):
            act.dma_start(att[:, :], attention.unsqueeze(0).to_broadcast([P, TYPES + 1])).then_inc(att_loaded, 16)
            for t in range(TYPES):
                k = slice(t * WIN, (t + 1) * WIN)
                act.dma_start(att_col[k, :], attention[t:t + 1].unsqueeze(0).to_broadcast([WIN, 1])).then_inc(att_loaded, 16)
                act.dma_start(brep[k, :], b_edge[t:t + 1, :].to_broadcast([WIN, D])).then_inc(wts_loaded, 16)
            act.dma_start(wts[:, :, :], w_edge.rearrange("t i o -> i t o")).then_inc(wts_loaded, 16)
            act.dma_start(wself[:, :], w_self[:, :]).then_inc(wts_loaded, 16)
            act.dma_start(bself[:, :], b_self.unsqueeze(1)).then_inc(wts_loaded, 16)
            act.wait_ge(prep_step, 1)
            nc.scalar.activation(att[:, :], att[:, :], ACT.Exp, bias=att_max[:, 1:2], accum_out=att_sum[:, 0:1])
            nc.scalar.activation(att_col[0:SW, :], att_col[0:SW, :], ACT.Exp, bias=att_max[0:SW, 1:2]).then_inc(exp_done, 1)

            def one_pass(p):
                for c in range(ROWC):
                    R = ROWS[c]
                    act.wait_ge(src_loaded[c], (p + 1) * (16 * SRC_DMAS[c]))
                    if c > 0:
                        act.wait_ge(srcT_done, p * ROWC + c)
                    nc.scalar.copy(srcf_row[0:R, :], src_row[0:R, c, :]).then_inc(srcf_ready, 1)
                    act.wait_ge(srcT_done, p * ROWC + c + 1)
                    nc.scalar.copy(src_all[:, c * P * TPG:(c * P + R) * TPG].rearrange("p (r j) -> p j r", j=TPG),
                                   agg[0][:, 0:TPG * R].rearrange("p (j r) -> p j r", j=TPG)).then_inc(srcT_copied, 1)
                    if c == 0:
                        act.wait_ge(srcT_copied, p * ROWC + 1)
                        for u in range(RING):
                            nc.scalar.copy(idx[:, u, :], src_all[:, u * TPG:(u + 1) * TPG]).then_inc(slot_free, 1)
                act.wait_ge(srcT_copied, (p + 1) * ROWC)
                act.wait_ge(keyT_copied, (p + 1) * ROWC)

                def step(it, u, g, with_block):
                    G = p * GROUPS + g
                    B = p * BLOCKS + it
                    n = tiles(g)
                    if there(g):
                        if late(g):
                            act.wait_ge(select_ready, G - (RING - 1))
                        nc.scalar.copy(meta[:, u, :], meta_all[:, ds(g * (2 * TPG), 2 * TPG)]).then_inc(meta_ready, 1)
                        act.wait_ge(stats_ready, G + 1)
                        if late(g):
                            act.wait_ge(summed, G - (RING - 1))
                        m = n + 1 if with_block and u == 0 else n
                        nc.scalar.activation(std[:, u, 0:m], meanvar[:, u, 0:m, 1], ACT.Sqrt,
                                             bias=eps[:, 0:1]).then_inc(std_ready, 1)
                        if with_block and u == 0:
                            if not isinstance(it, int) or it > 0:
                                act.wait_ge(selfT_done, B)
                            nc.scalar.activation(hid_self[:, :], xres[:, ds(it * D, D)], ACT.Relu,
                                                 bias=negmean[:, u, SELF:SELF + 1])
                        for j in range(n):
                            last = nc.scalar.activation(hid[:, u, j, :], raw[:, u, j * D:(j + 1) * D], ACT.Relu,
                                                        bias=negmean[:, u, j:j + 1])
                        last.then_inc(hid_ready, 1)
                        if not isinstance(g, int) or g + RING < GROUPS:
                            act.wait_ge(hid_ready, G + 1)
                            nc.scalar.copy(idx[:, u, :], src_all[:, ds((g + RING) * TPG, TPG)]).then_inc(slot_free, 1)
                    if with_block and u == 1:
                        act.wait_ge(selfT_done, B + 1)
                        if not isinstance(it, int) or it > 0:
                            act.wait_ge(self_done, B)
                        nc.scalar.copy(hidT_self[:, :], selfT[:, 0:P]).then_inc(selfT_ready, 1)
                    k, v = g - 2, (u - 2) % RING
                    if there(k):
                        act.wait_ge(summed, G - 1)
                        if late(k):
                            act.wait_ge(weighted, G - 2 - (RING - 1))
                        nc.scalar.copy(sums[:, v, :], agg[v][:, 0:SW]).then_inc(sums_ready, 1)

                walk(act, step)

            passes(act, one_pass)

            def out_step(o, k, later):
                if later:
                    act.wait_ge(gelT_done, o - 1)
                nc.scalar.activation(gel[:, k, :], acc[:, ds(o * (OUTB * P), OUTB * P)], ACT.Gelu).then_inc(gel_ready, 1)

            act.wait_ge(acc_final, 1)
            out_step(0, 0, False)
            out_step(1, 1, False)
            with act.Fori(2, OSTEPS - 1, 2) as o:
                out_step(o, 0, True)
                out_step(o + 1, 1, True)

        @block.vector
        def _(dve):
            dve.wait_ge(att_loaded, 16 * (TYPES + 1))
            nc.vector.tensor_reduce(out=att_max[:, 0:1], in_=att[:, :], axis=AX.X, op=ALU.max).then_inc(max_done, 1)
            dve.wait_ge(max_done, 1)
            nc.vector.tensor_scalar(att_max[:, 1:2], att_max[:, 0:1], -1.0, None, ALU.mult).then_inc(prep_step, 1)
            dve.wait_ge(exp_done, 1)
            nc.vector.reciprocal(att_sum[:, 1:2], att_sum[:, 0:1]).then_inc(prep_step, 1)
            dve.wait_ge(prep_step, 2)
            nc.vector.tensor_scalar(att[:, :], att[:, :], att_sum[:, 1:2], None, ALU.mult)
            nc.vector.tensor_scalar(att_col[0:SW, :], att_col[0:SW, :], att_sum[0:SW, 1:2], None, ALU.mult).then_inc(prep_step, 1)
            dve.wait_ge(prep_step, 3)
            dve.wait_ge(wts_loaded, 16 * (TYPES + 3))
            for t in range(TYPES):
                nc.vector.tensor_scalar(wts[:, t, :], wts[:, t, :], att[:, t:t + 1], None, ALU.mult)
            nc.vector.tensor_scalar(wself[:, :], wself[:, :], att[:, TYPES:TYPES + 1], None, ALU.mult)
            nc.vector.tensor_scalar(bself[:, :], bself[:, :], att[:, TYPES:TYPES + 1], None, ALU.mult)
            nc.vector.tensor_scalar(brep[0:SW, :], brep[0:SW, :], att_col[0:SW, 0:1], None, ALU.mult).then_inc(weights_ready, 1)
            dve.wait_ge(consts_ready, 1)

            ORDER = 3

            def one_pass(p):
                dve.wait_ge(weights_ready, p + 1)
                for c in range(ROWC):
                    R = ROWS[c]
                    S = p * (ORDER * ROWC) + ORDER * c
                    d = dst_row[0:R, c, :]
                    dve.wait_ge(row_loaded[c], (p + 1) * (16 * ROW_DMAS[c]))
                    nc.vector.tensor_reduce(out=first_dst[0:R, 0:1], in_=d, axis=AX.X, op=ALU.min)
                    nc.vector.tensor_reduce(out=first_dst[0:R, 1:2], in_=d, axis=AX.X, op=ALU.max).then_inc(row_step, 1)
                    dve.wait_ge(row_step, S + 1)
                    if c > 0:
                        dve.wait_ge(keyT_done, p * ROWC + c)
                    nc.vector.tensor_scalar(base_col[0:R, 0:1], first_dst[0:R, 0:1], shift[0:R, 0:1], float(NODES), ALU.add, ALU.min)
                    nc.vector.tensor_tensor(base_col[0:R, 1:2], first_dst[0:R, 1:2], first_dst[0:R, 0:1], ALU.subtract).then_inc(row_step, 1)
                    dve.wait_ge(row_step, S + 2)
                    nc.vector.tensor_scalar(first_dst[0:R, 2:3], base_col[0:R, 0:1], -1.0, None, ALU.add)
                    nc.vector.tensor_scalar(first_dst[0:R, 3:4], base_col[0:R, 0:1], float(WIN), None, ALU.add).then_inc(row_step, 1)
                    dve.wait_ge(row_step, S + 3)
                    nc.vector.tensor_scalar(rel_row[0:R, :], d, first_dst[0:R, 2:3], None, ALU.subtract).then_inc(key_step, 1)
                    dve.wait_ge(key_step, p * (2 * ROWC) + 2 * c + 1)
                    nc.vector.scalar_tensor_tensor(side_row[0:R, :], d, first_dst[0:R, 3:4], rel_row[0:R, :], ALU.subtract, ALU.mult)
                    nc.vector.scalar_tensor_tensor(typ1_row[0:R, :], typ_row[0:R, c, :], float(WIN), rel_row[0:R, :], ALU.mult, ALU.add).then_inc(key_step, 1)
                    dve.wait_ge(key_step, p * (2 * ROWC) + 2 * c + 2)
                    nc.vector.scalar_tensor_tensor(key_row[0:R, :], side_row[0:R, :], 0.0, typ1_row[0:R, :], ALU.is_lt, ALU.mult).then_inc(key_ready, 1)
                    dve.wait_ge(keyT_done, p * ROWC + c + 1)
                    m = meta_all[:, c * P * 2 * TPG:(c * P + R) * 2 * TPG].rearrange("p (r s j) -> p s j r", s=2, j=TPG)
                    nc.vector.tensor_copy(m[:, 0], agg[1][:, 0:TPG * R].rearrange("p (j r) -> p j r", j=TPG))
                    nc.vector.tensor_copy(m[:, 1], agg[2][:, 0:TPG * R].rearrange("p (j r) -> p j r", j=TPG))
                    nc.vector.tensor_copy(base_row[0:1, c * P:c * P + R], selfT[0:1, 0:R])
                    nc.vector.tensor_copy(span_row[0:1, c * P:c * P + R], selfT[0:1, P:P + R]).then_inc(keyT_copied, 1)
                dve.wait_ge(keyT_copied, (p + 1) * ROWC)
                nc.vector.tensor_reduce(out=span_max[0:1, 0:1], in_=span_row[0:1, :], axis=AX.X, op=ALU.max).then_inc(span_ready, 1)

                def step(it, u, g, with_block):
                    G = p * GROUPS + g
                    B = p * BLOCKS + it
                    if there(g):
                        n = tiles(g)
                        m = n
                        if late(g):
                            dve.wait_ge(hid_ready, G - (RING - 1))
                        if with_block and u == 0:
                            m = n + 1
                            dve.wait_ge(x_loaded, it * 16 + 16)
                            nc.vector.bn_stats(out=stats[:, u, SELF, :], in_=xres[:, ds(it * D, D)])
                        dve.wait_ge(gathered[u], p * GATHER_INC[u] + (it * (16 * TPG) + 16 * n))
                        for j in range(n):
                            last = nc.vector.bn_stats(out=stats[:, u, j, :], in_=raw[:, u, j * D:(j + 1) * D])
                        last.then_inc(bn_done, 1)
                        dve.wait_ge(bn_done, G + 1)
                        settle(dve)
                        for j in range(m):
                            last = nc.vector.bn_aggr(out=meanvar[:, u, j, :], in_=stats[:, u, j, :])
                        last.then_inc(aggr_done, 1)
                        dve.wait_ge(aggr_done, G + 1)
                        nc.vector.tensor_scalar(negmean[:, u, 0:m], meanvar[:, u, 0:m, 0], -1.0, None, ALU.mult).then_inc(stats_ready, 1)
                    k, v = g - 1, (u - 1) % RING
                    if there(k):
                        n = tiles(k)
                        m = n + 1 if with_block and v == 0 else n
                        dve.wait_ge(std_ready, G)
                        nc.vector.reciprocal(rstd[:, v, 0:m], std[:, v, 0:m]).then_inc(rstd_done, 1)
                        dve.wait_ge(rstd_done, G)
                        dve.wait_ge(meta_ready, G)
                        nc.vector.tensor_tensor(scale[:, v, 0:n], meta[:, v, TPG:TPG + n], rstd[:, v, 0:n], ALU.mult).then_inc(scale_done, 1)
                        if m > n:
                            if not isinstance(it, int) or it > 0:
                                dve.wait_ge(selfT_done, B)
                            nc.vector.tensor_scalar(diag[:, :], ident[:, :], rstd[:, v, SELF:SELF + 1], None, ALU.mult)
                        dve.wait_ge(scale_done, G)
                        if late(k):
                            dve.wait_ge(summed, G - 1 - (RING - 1))
                        for j in range(n):
                            last = nc.vector.tensor_scalar(select[:, v, j, :], iota[:, :], meta[:, v, j:j + 1],
                                                           scale[:, v, j:j + 1], ALU.is_equal, ALU.mult)
                        last.then_inc(select_ready, 1)
                    k, v = g - 2, (u - 2) % RING
                    if there(k):
                        dve.wait_ge(summed, G - 1)
                        if late(k):
                            dve.wait_ge(weighted, G - 2 - (RING - 1))
                        nc.vector.tensor_scalar(wsum[0:SW, v, :], fold[0:SW, :], co[v][0:SW, 0:1], None, ALU.mult).then_inc(wsum_ready, 1)
                    if with_block and u == 2:
                        dve.wait_ge(self_done, B + 1)
                        if isinstance(it, int) and it == 0:
                            dve.wait_ge(acc_zeroed, 16)
                        else:
                            dve.wait_ge(acc_added, G - 3)
                        nc.vector.scalar_tensor_tensor(acc[:, ds(it * P, P)], selfO[:, 0:P], bself[:, 0:1],
                                                       acc[:, ds(it * P, P)], ALU.add, ALU.add).then_inc(self_added, 1)
                    k, v = g - 3, u
                    if there(k):
                        base = dve.value_load(base_row[0:1, ds(k, 1)], min_val=0, max_val=NODES)
                        dve.wait_ge(weighted, G - 2)
                        if with_block and u == 2:
                            dve.wait_ge(self_added, B + 1)
                        if not isinstance(k, int) or k > 0:
                            dve.wait_ge(acc_added, G - 3)
                        nc.vector.tensor_tensor(acc[:, ds(base, WIN)], acc[:, ds(base, WIN)],
                                                co[v][:, OUT0:OUT0 + WIN], ALU.add).then_inc(acc_added, 1)

                walk(dve, step)
                dve.wait_ge(acc_added, (p + 1) * GROUPS)
                nc.vector.tensor_scalar(shift[:, :], shift[:, :], float(WIN), None, ALU.add)
                nc.vector.memset(wself[:, :], 0.0)
                nc.vector.memset(bself[:, :], 0.0).then_inc(weights_ready, 1)

            passes(dve, one_pass)
            nc.vector.drain().then_inc(acc_final, 1)

            def out_step(o, k):
                dve.wait_ge(gelT_done, o + 1)
                lo, n0, n1 = o * (OUTB * D), SPLIT * D, (OUTB - SPLIT) * D
                nc.vector.tensor_tensor(xres[:, ds(lo, n0)], xres[:, ds(lo, n0)], agg[k][:, 0:n0], ALU.add)
                nc.vector.tensor_tensor(xres[:, ds(lo + n0, n1)], xres[:, ds(lo + n0, n1)], co[k][:, 0:n1], ALU.add).then_inc(out_ready, 1)

            with dve.Fori(0, OSTEPS - 1, 2) as o:
                out_step(o, 0)
                out_step(o + 1, 1)

        @block.tensor
        def _(pe):
            pe.wait_ge(consts_ready, 1)

            def one_pass(p):
                for c in range(ROWC):
                    R = ROWS[c]
                    C = p * ROWC + c
                    pe.wait_ge(srcf_ready, C + 1)
                    if c > 0:
                        pe.wait_ge(srcT_copied, C)
                    settle(pe)
                    for j in range(TPG):
                        last = nc.tensor.transpose(agg[0][:, j * R:(j + 1) * R], srcf_row[0:R, j * P:(j + 1) * P], ident[0:R, 0:R])
                    last.then_inc(srcT_done, 1)
                    pe.wait_ge(key_ready, C + 1)
                    if c > 0:
                        pe.wait_ge(keyT_copied, C)
                    settle(pe)
                    for j in range(TPG):
                        nc.tensor.transpose(agg[1][:, j * R:(j + 1) * R], key_row[0:R, j * P:(j + 1) * P], ident[0:R, 0:R])
                        nc.tensor.transpose(agg[2][:, j * R:(j + 1) * R], ew_row[0:R, c, j * P:(j + 1) * P], ident[0:R, 0:R])
                    nc.tensor.transpose(selfT[0:1, 0:R], base_col[0:R, 0:1], ident[0:R, 0:R])
                    nc.tensor.transpose(selfT[0:1, P:P + R], base_col[0:R, 1:2], ident[0:R, 0:R]).then_inc(keyT_done, 1)
                pe.wait_ge(srcT_copied, (p + 1) * ROWC)
                pe.wait_ge(keyT_copied, (p + 1) * ROWC)
                pe.wait_ge(weights_ready, p + 1)

                def step(it, u, g, with_block):
                    G = p * GROUPS + g
                    B = p * BLOCKS + it
                    if with_block and u == 1:
                        pe.wait_ge(selfT_ready, B + 1)
                        if not isinstance(it, int) or it > 0:
                            pe.wait_ge(self_added, B)
                        nc.tensor.matmul(selfO[:, 0:P], wself[:, :], hidT_self[:, :], start=True, stop=True).then_inc(self_done, 1)
                    if there(g):
                        n = tiles(g)
                        pe.wait_ge(hid_ready, G + 1)
                        pe.wait_ge(select_ready, G + 1)
                        if late(g):
                            pe.wait_ge(sums_ready, G - (RING - 1))
                            pe.wait_ge(acc_added, G - (RING - 1))
                        for j in range(n):
                            nc.tensor.matmul(agg[u][:, 0:SW], hid[:, u, j, :], select[:, u, j, :], start=j == 0, stop=j == n - 1)
                            last = nc.tensor.matmul(co[u][0:SW, 0:1], select[:, u, j, :], std[:, u, j:j + 1], start=j == 0, stop=j == n - 1)
                        last.then_inc(summed, 1)
                        if with_block and u == 0:
                            if not isinstance(it, int) or it > 0:
                                pe.wait_ge(selfT_ready, B)
                            nc.tensor.matmul(selfT[:, 0:P], hid_self[:, :], diag[:, :], start=True, stop=True).then_inc(selfT_done, 1)
                    k, v = g - 1, (u - 1) % RING
                    if there(k):
                        pe.wait_ge(sums_ready, G)
                        pe.wait_ge(wsum_ready, G)
                        for t in range(TYPES):
                            nc.tensor.matmul(co[v][:, OUT0:OUT0 + WIN], wts[:, t, :], sums[:, v, t * WIN:(t + 1) * WIN],
                                             start=t == 0, stop=False)
                        nc.tensor.matmul(co[v][:, OUT0:OUT0 + WIN], brep[0:SW, :], wsum[0:SW, v, :],
                                         start=False, stop=True).then_inc(weighted, 1)

                walk(pe, step)

            passes(pe, one_pass)

            def out_step(o, k, later):
                pe.wait_ge(gel_ready, o + 1)
                if later:
                    pe.wait_ge(out_ready, o - 1)
                for b in range(OUTB):
                    to = agg[k][:, b * P:(b + 1) * P] if b < SPLIT else co[k][:, (b - SPLIT) * P:(b - SPLIT + 1) * P]
                    last = nc.tensor.transpose(to, gel[:, k, b * P:(b + 1) * P], ident[:, :])
                last.then_inc(gelT_done, 1)

            out_step(0, 0, False)
            out_step(1, 1, False)
            with pe.Fori(2, OSTEPS - 1, 2) as o:
                out_step(o, 0, True)
                out_step(o + 1, 1, True)


_INS = ["x", "src", "dst", "edge_type_3", "edge_weight", "L0_gnn_W_edge", "L0_gnn_b_edge", "L0_gnn_W_self",
        "L0_gnn_b_self", "L0_gnn_attention"]


def kernel(**inputs):
    import numpy as np
    import concourse.bacc as bacc
    from concourse.bass_utils import run_bass_kernel_spmd

    nc = bacc.Bacc("TRN2", target_bir_lowering=False, num_devices=1)
    arrays, args = {}, []
    for name in _INS:
        a = np.ascontiguousarray(inputs[name])
        arrays[f"in_{name}_dram"] = a
        args.append(nc.dram_tensor(f"in_{name}_dram", a.shape, mybir.dt.from_np(a.dtype), kind="ExternalInput").ap())
    shape = arrays["in_x_dram"].shape
    args.append(nc.dram_tensor("out_dram", shape, mybir.dt.float32, kind="ExternalOutput").ap())
    gnn_layer(nc, *args)
    r = run_bass_kernel_spmd(nc, [arrays], core_ids=[0])
    return r.results[0]["out_dram"]
```

```python
import concourse.bass as bass
from concourse import mybir
from contextlib import ExitStack


def gnn_layer(nc, x, src, dst, edge_type, edge_weight, w_edge, b_edge, w_self, b_self, attention, out):
    fp32 = mybir.dt.float32
    i32 = mybir.dt.int32
    ALU = mybir.AluOpType
    ACT = mybir.ActivationFunctionType
    AX = mybir.AxisListType
    ds = bass.ds

    P = 128
    NODES, D = x.shape
    EDGES = src.shape[0]
    TYPES = w_edge.shape[0]
    TPG = 4
    GE = TPG * P
    GROUPS = -(-EDGES // GE)
    LAST_EDGES = EDGES - (GROUPS - 1) * GE
    LAST_TILES = -(-LAST_EDGES // P)
    RING = 3
    ITERS = (GROUPS - 1) // RING
    assert ITERS * RING == GROUPS - 1
    WIN = 42
    SW = TYPES * WIN
    BLOCKS = -(-NODES // P)
    LAST_ROWS = NODES - (BLOCKS - 1) * P
    COLS = BLOCKS * P
    assert NODES + WIN <= COLS and BLOCKS < ITERS
    EPS = 1e-5
    ROWC = -(-GROUPS // P)
    ROWS = [min(P, GROUPS - c * P) for c in range(ROWC)]
    SELF = TPG
    OUTB = 7
    OSTEPS = BLOCKS // OUTB
    assert OSTEPS * OUTB == BLOCKS and OSTEPS % 2 == 0
    SPLIT = 4

    ctx = ExitStack()
    with ctx:
        def sb(name, shape, dt=fp32):
            return ctx.enter_context(nc.sbuf_tensor(name, shape, dt))

        def sem(name):
            return ctx.enter_context(nc.semaphore(name))

        acc = sb("acc", [P, COLS])
        xres = sb("xres", [P, BLOCKS * D])
        src_row = sb("src_row", [P, ROWC, GE], i32)
        dst_row = sb("dst_row", [P, ROWC, GE], i32)
        typ_row = sb("typ_row", [P, ROWC, GE], i32)
        ew_row = sb("ew_row", [P, ROWC, GE])
        srcf_row = sb("srcf_row", [P, GE])
        rel_row = sb("rel_row", [P, GE])
        side_row = sb("side_row", [P, GE])
        typ1_row = sb("typ1_row", [P, GE])
        key_row = sb("key_row", [P, GE])
        first_dst = sb("first_dst", [P, 4])
        base_col = sb("base_col", [P, 2])
        shift = sb("shift", [P, 1])
        src_all = sb("src_all", [P, GROUPS * TPG])
        meta_all = sb("meta_all", [P, GROUPS * 2 * TPG])
        base_row = sb("base_row", [1, GROUPS], i32)
        span_row = sb("span_row", [1, GROUPS])
        span_max = sb("span_max", [1, 1], i32)
        idx = sb("idx", [P, RING, TPG], i32)
        meta = sb("meta", [P, RING, 2 * TPG])
        raw = sb("raw", [P, RING, TPG * D])
        stats = sb("stats", [P, RING, TPG + 1, 6])
        meanvar = sb("meanvar", [P, RING, TPG + 1, 2])
        negmean = sb("negmean", [P, RING, TPG + 1])
        std = sb("std", [P, RING, TPG + 1])
        rstd = sb("rstd", [P, RING, TPG + 1])
        scale = sb("scale", [P, RING, TPG])
        hid = sb("hid", [P, RING, TPG, D])
        select = sb("select", [P, RING, TPG, SW])
        sums = sb("sums", [P, 2, TYPES, RING, WIN])
        hid_self = sb("hid_self", [P, D])
        diag = sb("diag", [P, P])
        hidT_self = sb("hidT_self", [P, P])
        gel = sb("gel", [P, 2, OUTB * P])
        ident = sb("ident", [P, P])
        iota_i = sb("iota_i", [P, SW], i32)
        iota = sb("iota", [P, SW])
        zeros = sb("zeros", [P, COLS // 16])
        eps = sb("eps", [P, 1])
        wts = sb("wts", [P, TYPES, D])
        wself = sb("wself", [P, D])
        bias = sb("bias", [P, TYPES, D])
        bself = sb("bself", [P, 1])
        att = sb("att", [P, TYPES + 1])
        att_max = sb("att_max", [P, 2])
        att_sum = sb("att_sum", [P, 2])

        def bank(name):
            return ctx.enter_context(nc.psum_tensor(name, [P, 512], fp32))

        agg = [bank(f"agg{i}") for i in range(RING)]
        through = bank("through")
        selfT = bank("selfT")
        selfO = bank("selfO")
        out2 = [through, selfT]

        consts_ready = sem("consts_ready")
        pool_step = sem("pool_step")
        att_loaded = sem("att_loaded")
        wts_loaded = sem("wts_loaded")
        acc_zeroed = sem("acc_zeroed")
        x_loaded = sem("x_loaded")
        prep_step = sem("prep_step")
        exp_done = sem("exp_done")
        max_done = sem("max_done")
        bias_zeroed = sem("bias_zeroed")
        acc_final = sem("acc_final")
        settled = sem("settled")
        weights_ready = sem("weights_ready")
        span_ready = sem("span_ready")
        src_loaded = [sem(f"src_loaded{c}") for c in range(ROWC)]
        row_loaded = [sem(f"row_loaded{c}") for c in range(ROWC)]
        srcf_ready = sem("srcf_ready")
        srcT_done = sem("srcT_done")
        srcT_copied = sem("srcT_copied")
        row_step = sem("row_step")
        key_step = sem("key_step")
        key_ready = sem("key_ready")
        keyT_done = sem("keyT_done")
        keyT_copied = sem("keyT_copied")
        slot_free = sem("slot_free")
        gathered = [sem(f"gathered{u}") for u in range(RING)]
        meta_ready = sem("meta_ready")
        bn_done = sem("bn_done")
        aggr_done = sem("aggr_done")
        stats_ready = sem("stats_ready")
        std_ready = sem("std_ready")
        rstd_done = sem("rstd_done")
        scale_done = sem("scale_done")
        hid_ready = sem("hid_ready")
        select_ready = sem("select_ready")
        summed = sem("summed")
        sums_ready = sem("sums_ready")
        acc_added = sem("acc_added")
        weighted = sem("weighted")
        selfT_done = sem("selfT_done")
        selfT_ready = sem("selfT_ready")
        self_done = sem("self_done")
        self_added = sem("self_added")
        gel_ready = sem("gel_ready")
        gelT_done = sem("gelT_done")
        out_ready = sem("out_ready")
        out_stored = sem("out_stored")

        SRC_DMAS = [1] * (ROWC - 1) + [3]
        ROW_DMAS = [3] * (ROWC - 1) + [8]
        GATHER_INC = [16 * TPG * ITERS + (16 * LAST_TILES if u == 0 else 0) for u in range(RING)]

        def settle(eng):
            eng.sem_inc(settled, 1)

        def tiles(g):
            return LAST_TILES if isinstance(g, int) and g == GROUPS - 1 else TPG

        def there(g):
            return not isinstance(g, int) or 0 <= g < GROUPS

        def late(g):
            return not isinstance(g, int) or g >= RING

        def walk(eng, step):
            for g in range(2 * RING):
                step(g // RING, g % RING, g, True)
            with eng.Fori(2, BLOCKS) as it:
                g0 = eng.snap(it * RING)
                for u in range(RING):
                    step(it, u, g0 + u, True)
            for g in range(BLOCKS * RING, (BLOCKS + 1) * RING):
                step(g // RING, g % RING, g, False)
            with eng.Fori(BLOCKS + 1, ITERS - 1) as it:
                g0 = eng.snap(it * RING)
                for u in range(RING):
                    step(it, u, g0 + u, False)
            for g in range((ITERS - 1) * RING, (ITERS + 2) * RING + 1):
                step(g // RING, g % RING, g, False)

        def passes(eng, body):
            limit = eng.alloc_register("pass_limit")
            eng.reg_mov(limit, 1)
            with eng.Fori(0, limit) as p:
                body(p)
                eng.wait_ge(span_ready, p + 1)
                settle(eng)
                eng.load(limit, span_max[0:1, 0:1])
                eng.reg_div(limit, limit, WIN)
                eng.reg_add(limit, limit, 1)

        block = ctx.enter_context(nc.Block())

        @block.sync
        def _(sp):
            def one_pass(p):
                for c in range(ROWC - 1):
                    lo, hi = c * P * GE, (c + 1) * P * GE
                    sp.dma_start(src_row[:, c, :], src[lo:hi].rearrange("(p e) -> p e", p=P)).then_inc(src_loaded[c], 16)
                    sp.dma_start(dst_row[:, c, :], dst[lo:hi].rearrange("(p e) -> p e", p=P)).then_inc(row_loaded[c], 16)
                    sp.dma_start(typ_row[:, c, :], edge_type[lo:hi].rearrange("(p e) -> p e", p=P)).then_inc(row_loaded[c], 16)
                    sp.dma_start(ew_row[:, c, :], edge_weight[lo:hi].rearrange("(p e) -> p e", p=P)).then_inc(row_loaded[c], 16)
                c, n = ROWC - 1, ROWS[-1] - 1
                lo, hi = c * P * GE, (GROUPS - 1) * GE
                fill = GE - LAST_EDGES
                sp.wait_ge(consts_ready, 1)
                for a, rows, signal in ((src, src_row, src_loaded[c]), (dst, dst_row, row_loaded[c]),
                                        (edge_type, typ_row, row_loaded[c]), (edge_weight, ew_row, row_loaded[c])):
                    sp.dma_start(rows[0:n, c, :], a[lo:hi].rearrange("(p e) -> p e", p=n)).then_inc(signal, 16)
                    sp.dma_start(rows[n:n + 1, c, 0:LAST_EDGES], a[hi:EDGES].rearrange("(p e) -> p e", p=1)).then_inc(signal, 16)
                    if a is not edge_weight:
                        sp.dma_start(rows[n:n + 1, c, LAST_EDGES:GE], a[EDGES - fill:EDGES].rearrange("(p e) -> p e", p=1)).then_inc(signal, 16)
                with sp.If(p < 1):
                    sp.dma_start(acc[:, :].rearrange("p (r c) -> p r c", r=16),
                                 zeros[:, :].unsqueeze(1).to_broadcast([P, 16, COLS // 16])).then_inc(acc_zeroed, 16)
                    sp.dma_start(xres[:, 0:D], x[0:P, :]).then_inc(x_loaded, 16)
                    with sp.Fori(1, BLOCKS - 1) as b:
                        sp.wait_ge(x_loaded, b * 16)
                        sp.dma_start(xres[:, ds(b * D, D)], x[ds(b * P, P), :]).then_inc(x_loaded, 16)
                    sp.wait_ge(x_loaded, (BLOCKS - 1) * 16)
                    sp.dma_start(xres[0:LAST_ROWS, (BLOCKS - 1) * D:], x[(BLOCKS - 1) * P:, :]).then_inc(x_loaded, 16)
                sp.wait_ge(acc_added, (p + 1) * GROUPS)

            passes(sp, one_pass)

            with sp.Fori(0, OSTEPS - 1) as o:
                sp.wait_ge(out_ready, o + 1)
                sp.dma_start(out[ds(o * (OUTB * P), OUTB * P), :].rearrange("(b p) d -> p b d", p=P),
                             xres[:, ds(o * (OUTB * D), OUTB * D)].rearrange("p (b d) -> p b d", d=D)).then_inc(out_stored, 16)
            sp.wait_ge(out_ready, OSTEPS)
            b0 = (OSTEPS - 1) * OUTB
            sp.dma_start(out[b0 * P:(BLOCKS - 1) * P, :].rearrange("(b p) d -> p b d", p=P),
                         xres[:, b0 * D:(BLOCKS - 1) * D].rearrange("p (b d) -> p b d", d=D)).then_inc(out_stored, 16)
            sp.dma_start(out[(BLOCKS - 1) * P:, :], xres[0:LAST_ROWS, (BLOCKS - 1) * D:]).then_inc(out_stored, 16)
            sp.wait_ge(out_stored, 16 * (OSTEPS + 1))

        @block.gpsimd
        def _(pool):
            nc.gpsimd.memset(ew_row[:, ROWC - 1, :], 0.0)
            nc.gpsimd.memset(xres[:, (BLOCKS - 1) * D:], 0.0)
            nc.gpsimd.memset(zeros[:, :], 0.0)
            nc.gpsimd.memset(eps[:, :], EPS)
            nc.gpsimd.memset(shift[:, :], 0.0)
            nc.gpsimd.iota(iota_i[:, :], pattern=[[1, SW]], base=1, channel_multiplier=0)
            nc.gpsimd.memset(ident[:, :], 0.0).then_inc(pool_step, 1)
            pool.wait_ge(pool_step, 1)
            nc.gpsimd.affine_select(out=ident[:, :], in_=ident[:, :], compare_op=ALU.not_equal, fill=1.0,
                                    base=0, pattern=[[-1, P]], channel_multiplier=1)
            nc.gpsimd.tensor_copy(iota[:, :], iota_i[:, :])
            nc.gpsimd.drain().then_inc(consts_ready, 1)

            def one_pass(p):
                def step(it, u, g, with_block):
                    if not there(g):
                        return
                    pool.wait_ge(slot_free, p * GROUPS + g + 1)
                    settle(pool)
                    for j in range(tiles(g)):
                        nc.gpsimd.indirect_dma_start(
                            raw[:, u, j * D:(j + 1) * D], None, x[:, :],
                            bass.IndirectOffsetOnAxis(ap=idx[:, u, j:j + 1], axis=0)).then_inc(gathered[u], 16)

                walk(pool, step)

            passes(pool, one_pass)

        @block.scalar
        def _(act):
            act.dma_start(att[:, :], attention.unsqueeze(0).to_broadcast([P, TYPES + 1])).then_inc(att_loaded, 16)
            act.dma_start(wts[:, :, :], w_edge.rearrange("t i o -> i t o")).then_inc(wts_loaded, 16)
            act.dma_start(wself[:, :], w_self[:, :]).then_inc(wts_loaded, 16)
            act.dma_start(bself[:, :], b_self.unsqueeze(1)).then_inc(wts_loaded, 16)
            act.wait_ge(bias_zeroed, 1)
            act.dma_start(bias[0:1, :, :], b_edge.unsqueeze(0)).then_inc(wts_loaded, 16)
            act.wait_ge(prep_step, 1)
            nc.scalar.activation(att[:, :], att[:, :], ACT.Exp, bias=att_max[:, 1:2], accum_out=att_sum[:, 0:1]).then_inc(exp_done, 1)

            def one_pass(p):
                for c in range(ROWC):
                    R = ROWS[c]
                    act.wait_ge(src_loaded[c], (p + 1) * (16 * SRC_DMAS[c]))
                    if c > 0:
                        act.wait_ge(srcT_done, p * ROWC + c)
                    nc.scalar.copy(srcf_row[0:R, :], src_row[0:R, c, :]).then_inc(srcf_ready, 1)
                    act.wait_ge(srcT_done, p * ROWC + c + 1)
                    nc.scalar.copy(src_all[:, c * P * TPG:(c * P + R) * TPG].rearrange("p (r j) -> p j r", j=TPG),
                                   agg[0][:, 0:TPG * R].rearrange("p (j r) -> p j r", j=TPG)).then_inc(srcT_copied, 1)
                    if c == 0:
                        act.wait_ge(srcT_copied, p * ROWC + 1)
                        for u in range(RING):
                            nc.scalar.copy(idx[:, u, :], src_all[:, u * TPG:(u + 1) * TPG]).then_inc(slot_free, 1)
                act.wait_ge(srcT_copied, (p + 1) * ROWC)
                act.wait_ge(keyT_copied, (p + 1) * ROWC)

                def step(it, u, g, with_block):
                    G = p * GROUPS + g
                    B = p * BLOCKS + it
                    n = tiles(g)
                    if there(g):
                        if late(g):
                            act.wait_ge(select_ready, G - (RING - 1))
                        nc.scalar.copy(meta[:, u, :], meta_all[:, ds(g * (2 * TPG), 2 * TPG)]).then_inc(meta_ready, 1)
                        act.wait_ge(stats_ready, G + 1)
                        if late(g):
                            act.wait_ge(summed, G - (RING - 1))
                        m = n + 1 if with_block and u == 0 else n
                        nc.scalar.activation(std[:, u, 0:m], meanvar[:, u, 0:m, 1], ACT.Sqrt,
                                             bias=eps[:, 0:1]).then_inc(std_ready, 1)
                        if with_block and u == 0:
                            if not isinstance(it, int) or it > 0:
                                act.wait_ge(selfT_done, B)
                            nc.scalar.activation(hid_self[:, :], xres[:, ds(it * D, D)], ACT.Relu,
                                                 bias=negmean[:, u, SELF:SELF + 1])
                        for j in range(n):
                            last = nc.scalar.activation(hid[:, u, j, :], raw[:, u, j * D:(j + 1) * D], ACT.Relu,
                                                        bias=negmean[:, u, j:j + 1])
                        last.then_inc(hid_ready, 1)
                        if not isinstance(g, int) or g + RING < GROUPS:
                            act.wait_ge(hid_ready, G + 1)
                            nc.scalar.copy(idx[:, u, :], src_all[:, ds((g + RING) * TPG, TPG)]).then_inc(slot_free, 1)
                    if with_block and u == RING - 1:
                        act.wait_ge(selfT_done, B + 1)
                        if not isinstance(it, int) or it > 0:
                            act.wait_ge(self_done, B)
                        nc.scalar.copy(hidT_self[:, :], selfT[:, 0:P]).then_inc(selfT_ready, 1)
                    k, v = g - 2, (u - 2) % RING
                    if there(k):
                        act.wait_ge(summed, G - 1)
                        if v == 0 and (not isinstance(k, int) or k > 0):
                            act.wait_ge(weighted, p * (ITERS + 1) + it)
                        nc.scalar.copy(sums[:, :, :, v, :], agg[v][:, 0:2 * SW].rearrange(
                            "p (s t w) -> p s t w", s=2, t=TYPES)).then_inc(sums_ready, 1)

                walk(act, step)

            passes(act, one_pass)

            def out_step(o, k, later):
                if later:
                    act.wait_ge(gelT_done, o - 1)
                nc.scalar.activation(gel[:, k, :], acc[:, ds(o * (OUTB * P), OUTB * P)], ACT.Gelu).then_inc(gel_ready, 1)

            act.wait_ge(acc_final, 1)
            out_step(0, 0, False)
            out_step(1, 1, False)
            with act.Fori(2, OSTEPS - 1, 2) as o:
                out_step(o, 0, True)
                out_step(o + 1, 1, True)

        @block.vector
        def _(dve):
            nc.vector.memset(bias[:, :, :], 0.0).then_inc(bias_zeroed, 1)
            dve.wait_ge(att_loaded, 16)
            nc.vector.tensor_reduce(out=att_max[:, 0:1], in_=att[:, :], axis=AX.X, op=ALU.max).then_inc(max_done, 1)
            dve.wait_ge(max_done, 1)
            nc.vector.tensor_scalar(att_max[:, 1:2], att_max[:, 0:1], -1.0, None, ALU.mult).then_inc(prep_step, 1)
            dve.wait_ge(exp_done, 1)
            nc.vector.reciprocal(att_sum[:, 1:2], att_sum[:, 0:1]).then_inc(prep_step, 1)
            dve.wait_ge(prep_step, 2)
            nc.vector.tensor_scalar(att[:, :], att[:, :], att_sum[:, 1:2], None, ALU.mult).then_inc(prep_step, 1)
            dve.wait_ge(prep_step, 3)
            dve.wait_ge(wts_loaded, 16 * 4)
            for t in range(TYPES):
                nc.vector.tensor_scalar(wts[:, t, :], wts[:, t, :], att[:, t:t + 1], None, ALU.mult)
                nc.vector.tensor_scalar(bias[:, t, :], bias[:, t, :], att[:, t:t + 1], None, ALU.mult)
            nc.vector.tensor_scalar(wself[:, :], wself[:, :], att[:, TYPES:TYPES + 1], None, ALU.mult)
            nc.vector.tensor_scalar(bself[:, :], bself[:, :], att[:, TYPES:TYPES + 1], None, ALU.mult).then_inc(weights_ready, 1)
            dve.wait_ge(consts_ready, 1)

            ORDER = 3

            base_regs = [dve.alloc_register(f"base{v}") for v in range(RING)]

            def one_pass(p):
                dve.wait_ge(weights_ready, p + 1)
                for c in range(ROWC):
                    R = ROWS[c]
                    S = p * (ORDER * ROWC) + ORDER * c
                    d = dst_row[0:R, c, :]
                    dve.wait_ge(row_loaded[c], (p + 1) * (16 * ROW_DMAS[c]))
                    nc.vector.tensor_reduce(out=first_dst[0:R, 0:1], in_=d, axis=AX.X, op=ALU.min)
                    nc.vector.tensor_reduce(out=first_dst[0:R, 1:2], in_=d, axis=AX.X, op=ALU.max).then_inc(row_step, 1)
                    dve.wait_ge(row_step, S + 1)
                    if c > 0:
                        dve.wait_ge(keyT_done, p * ROWC + c)
                    nc.vector.tensor_scalar(base_col[0:R, 0:1], first_dst[0:R, 0:1], shift[0:R, 0:1], float(NODES), ALU.add, ALU.min)
                    nc.vector.tensor_tensor(base_col[0:R, 1:2], first_dst[0:R, 1:2], first_dst[0:R, 0:1], ALU.subtract).then_inc(row_step, 1)
                    dve.wait_ge(row_step, S + 2)
                    nc.vector.tensor_scalar(first_dst[0:R, 2:3], base_col[0:R, 0:1], -1.0, None, ALU.add)
                    nc.vector.tensor_scalar(first_dst[0:R, 3:4], base_col[0:R, 0:1], float(WIN), None, ALU.add).then_inc(row_step, 1)
                    dve.wait_ge(row_step, S + 3)
                    nc.vector.tensor_scalar(rel_row[0:R, :], d, first_dst[0:R, 2:3], None, ALU.subtract).then_inc(key_step, 1)
                    dve.wait_ge(key_step, p * (2 * ROWC) + 2 * c + 1)
                    nc.vector.scalar_tensor_tensor(side_row[0:R, :], d, first_dst[0:R, 3:4], rel_row[0:R, :], ALU.subtract, ALU.mult)
                    nc.vector.scalar_tensor_tensor(typ1_row[0:R, :], typ_row[0:R, c, :], float(WIN), rel_row[0:R, :], ALU.mult, ALU.add).then_inc(key_step, 1)
                    dve.wait_ge(key_step, p * (2 * ROWC) + 2 * c + 2)
                    nc.vector.scalar_tensor_tensor(key_row[0:R, :], side_row[0:R, :], 0.0, typ1_row[0:R, :], ALU.is_lt, ALU.mult).then_inc(key_ready, 1)
                    dve.wait_ge(keyT_done, p * ROWC + c + 1)
                    m = meta_all[:, c * P * 2 * TPG:(c * P + R) * 2 * TPG].rearrange("p (r s j) -> p s j r", s=2, j=TPG)
                    nc.vector.tensor_copy(m[:, 0], agg[1][:, 0:TPG * R].rearrange("p (j r) -> p j r", j=TPG))
                    nc.vector.tensor_copy(m[:, 1], agg[2][:, 0:TPG * R].rearrange("p (j r) -> p j r", j=TPG))
                    nc.vector.tensor_copy(base_row[0:1, c * P:c * P + R], selfT[0:1, 0:R])
                    nc.vector.tensor_copy(span_row[0:1, c * P:c * P + R], selfT[0:1, P:P + R]).then_inc(keyT_copied, 1)
                dve.wait_ge(keyT_copied, (p + 1) * ROWC)
                nc.vector.tensor_reduce(out=span_max[0:1, 0:1], in_=span_row[0:1, :], axis=AX.X, op=ALU.max).then_inc(span_ready, 1)

                def step(it, u, g, with_block):
                    G = p * GROUPS + g
                    B = p * BLOCKS + it
                    if there(g):
                        n = tiles(g)
                        m = n
                        if late(g):
                            dve.wait_ge(hid_ready, G - (RING - 1))
                        if with_block and u == 0:
                            m = n + 1
                            dve.wait_ge(x_loaded, it * 16 + 16)
                            nc.vector.bn_stats(out=stats[:, u, SELF, :], in_=xres[:, ds(it * D, D)])
                        dve.wait_ge(gathered[u], p * GATHER_INC[u] + (it * (16 * TPG) + 16 * n))
                        for j in range(n):
                            last = nc.vector.bn_stats(out=stats[:, u, j, :], in_=raw[:, u, j * D:(j + 1) * D])
                        last.then_inc(bn_done, 1)
                        dve.wait_ge(bn_done, G + 1)
                        settle(dve)
                        for j in range(m):
                            last = nc.vector.bn_aggr(out=meanvar[:, u, j, :], in_=stats[:, u, j, :])
                        last.then_inc(aggr_done, 1)
                        dve.wait_ge(aggr_done, G + 1)
                        nc.vector.tensor_scalar(negmean[:, u, 0:m], meanvar[:, u, 0:m, 0], -1.0, None, ALU.mult).then_inc(stats_ready, 1)
                    k, v = g - 1, (u - 1) % RING
                    if there(k):
                        n = tiles(k)
                        m = n + 1 if with_block and v == 0 else n
                        dve.wait_ge(std_ready, G)
                        nc.vector.reciprocal(rstd[:, v, 0:m], std[:, v, 0:m]).then_inc(rstd_done, 1)
                        dve.wait_ge(rstd_done, G)
                        dve.wait_ge(meta_ready, G)
                        nc.vector.tensor_tensor(scale[:, v, 0:n], meta[:, v, TPG:TPG + n], rstd[:, v, 0:n], ALU.mult).then_inc(scale_done, 1)
                        if m > n:
                            if not isinstance(it, int) or it > 0:
                                dve.wait_ge(selfT_done, B)
                            nc.vector.tensor_scalar(diag[:, :], ident[:, :], rstd[:, v, SELF:SELF + 1], None, ALU.mult)
                        dve.wait_ge(scale_done, G)
                        if late(k):
                            dve.wait_ge(summed, G - 1 - (RING - 1))
                        for j in range(n):
                            last = nc.vector.tensor_scalar(select[:, v, j, :], iota[:, :], meta[:, v, j:j + 1],
                                                           scale[:, v, j:j + 1], ALU.is_equal, ALU.mult)
                        last.then_inc(select_ready, 1)
                    if u == RING - 1 and (not isinstance(it, int) or 0 < it <= ITERS + 1):
                        groups = RING if not isinstance(it, int) or it <= ITERS else GROUPS - ITERS * RING
                        dve.load(base_regs[0:groups], base_row[0:1, ds((it - 1) * RING, groups)])
                    if u == 0 and (not isinstance(it, int) or 1 < it <= ITERS + 2):
                        groups = RING if not isinstance(it, int) or it < ITERS + 2 else GROUPS - ITERS * RING
                        dve.wait_ge(weighted, p * (ITERS + 1) + (it - 1))
                        if with_block or isinstance(it, int) and it - 2 < BLOCKS:
                            dve.wait_ge(self_added, B - 1)
                        for v in range(groups):
                            if v > 0 or not isinstance(it, int) or it > 2:
                                dve.wait_ge(acc_added, p * GROUPS + ((it - 2) * RING + v))
                            base = dve.snap(base_regs[v], min_val=0, max_val=NODES)
                            nc.vector.tensor_tensor(acc[:, ds(base, WIN)], acc[:, ds(base, WIN)],
                                                    through[:, v * WIN:(v + 1) * WIN], ALU.add).then_inc(acc_added, 1)
                    if u == 1 and (with_block and not (isinstance(it, int) and it == 0) or isinstance(it, int) and it == BLOCKS):
                        dve.wait_ge(self_done, B)
                        if isinstance(it, int) and it == 1:
                            dve.wait_ge(acc_zeroed, 16)
                        else:
                            dve.wait_ge(acc_added, p * GROUPS + (it - 1) * RING)
                        nc.vector.scalar_tensor_tensor(acc[:, ds((it - 1) * P, P)], selfO[:, 0:P], bself[:, 0:1],
                                                       acc[:, ds((it - 1) * P, P)], ALU.add, ALU.add).then_inc(self_added, 1)

                walk(dve, step)
                dve.wait_ge(acc_added, (p + 1) * GROUPS)
                nc.vector.tensor_scalar(shift[:, :], shift[:, :], float(WIN), None, ALU.add)
                nc.vector.memset(wself[:, :], 0.0)
                nc.vector.memset(bself[:, :], 0.0).then_inc(weights_ready, 1)

            passes(dve, one_pass)
            nc.vector.drain().then_inc(acc_final, 1)

            def out_step(o, k):
                dve.wait_ge(gelT_done, o + 1)
                lo, n0, n1 = o * (OUTB * D), SPLIT * D, (OUTB - SPLIT) * D
                nc.vector.tensor_tensor(xres[:, ds(lo, n0)], xres[:, ds(lo, n0)], agg[k][:, 0:n0], ALU.add)
                nc.vector.tensor_tensor(xres[:, ds(lo + n0, n1)], xres[:, ds(lo + n0, n1)], out2[k][:, 0:n1], ALU.add).then_inc(out_ready, 1)

            with dve.Fori(0, OSTEPS - 1, 2) as o:
                out_step(o, 0)
                out_step(o + 1, 1)

        @block.tensor
        def _(pe):
            pe.wait_ge(consts_ready, 1)

            def one_pass(p):
                for c in range(ROWC):
                    R = ROWS[c]
                    C = p * ROWC + c
                    pe.wait_ge(srcf_ready, C + 1)
                    if c > 0:
                        pe.wait_ge(srcT_copied, C)
                    settle(pe)
                    for j in range(TPG):
                        last = nc.tensor.transpose(agg[0][:, j * R:(j + 1) * R], srcf_row[0:R, j * P:(j + 1) * P], ident[0:R, 0:R])
                    last.then_inc(srcT_done, 1)
                    pe.wait_ge(key_ready, C + 1)
                    if c > 0:
                        pe.wait_ge(keyT_copied, C)
                    settle(pe)
                    for j in range(TPG):
                        nc.tensor.transpose(agg[1][:, j * R:(j + 1) * R], key_row[0:R, j * P:(j + 1) * P], ident[0:R, 0:R])
                        nc.tensor.transpose(agg[2][:, j * R:(j + 1) * R], ew_row[0:R, c, j * P:(j + 1) * P], ident[0:R, 0:R])
                    nc.tensor.transpose(selfT[0:1, 0:R], base_col[0:R, 0:1], ident[0:R, 0:R])
                    nc.tensor.transpose(selfT[0:1, P:P + R], base_col[0:R, 1:2], ident[0:R, 0:R]).then_inc(keyT_done, 1)
                pe.wait_ge(srcT_copied, (p + 1) * ROWC)
                pe.wait_ge(keyT_copied, (p + 1) * ROWC)
                pe.wait_ge(weights_ready, p + 1)

                def step(it, u, g, with_block):
                    G = p * GROUPS + g
                    B = p * BLOCKS + it
                    if u == 1 and (not isinstance(it, int) or 0 < it <= ITERS + 1):
                        done = p * GROUPS + (GROUPS if isinstance(it, int) and it == ITERS + 1 else it * RING)
                        pe.wait_ge(sums_ready, done)
                        if not isinstance(it, int) or it > 1:
                            pe.wait_ge(acc_added, p * GROUPS + (it - 1) * RING)
                        for t in range(TYPES):
                            nc.tensor.matmul(through[:, 0:SW], wts[:, t, :], sums[:, 0, t, :, :].rearrange("p u w -> p (u w)"),
                                             start=t == 0, stop=False)
                        for t in range(TYPES):
                            last = nc.tensor.matmul(through[:, 0:SW], bias[:, t, :], sums[:, 1, t, :, :].rearrange("p u w -> p (u w)"),
                                                    start=False, stop=t == TYPES - 1)
                        last.then_inc(weighted, 1)
                    if with_block and u == RING - 1:
                        pe.wait_ge(selfT_ready, B + 1)
                        if not isinstance(it, int) or it > 0:
                            pe.wait_ge(self_added, B)
                        nc.tensor.matmul(selfO[:, 0:P], wself[:, :], hidT_self[:, :], start=True, stop=True).then_inc(self_done, 1)
                    if there(g):
                        n = tiles(g)
                        pe.wait_ge(hid_ready, G + 1)
                        pe.wait_ge(select_ready, G + 1)
                        if late(g):
                            pe.wait_ge(sums_ready, G - (RING - 1))
                        for j in range(n):
                            nc.tensor.matmul(agg[u][:, 0:SW], hid[:, u, j, :], select[:, u, j, :], start=j == 0, stop=False)
                            last = nc.tensor.matmul(agg[u][:, SW:2 * SW], std[:, u, j:j + 1].to_broadcast([P, P]),
                                                    select[:, u, j, :], start=False, stop=j == n - 1)
                        last.then_inc(summed, 1)
                        if with_block and u == 0:
                            if not isinstance(it, int) or it > 0:
                                pe.wait_ge(selfT_ready, B)
                            nc.tensor.matmul(selfT[:, 0:P], hid_self[:, :], diag[:, :], start=True, stop=True).then_inc(selfT_done, 1)

                walk(pe, step)

            passes(pe, one_pass)

            def out_step(o, k, later):
                pe.wait_ge(gel_ready, o + 1)
                if later:
                    pe.wait_ge(out_ready, o - 1)
                for b in range(OUTB):
                    to = agg[k][:, b * P:(b + 1) * P] if b < SPLIT else out2[k][:, (b - SPLIT) * P:(b - SPLIT + 1) * P]
                    last = nc.tensor.transpose(to, gel[:, k, b * P:(b + 1) * P], ident[:, :])
                last.then_inc(gelT_done, 1)

            out_step(0, 0, False)
            out_step(1, 1, False)
            with pe.Fori(2, OSTEPS - 1, 2) as o:
                out_step(o, 0, True)
                out_step(o + 1, 1, True)


_INS = ["x", "src", "dst", "edge_type_3", "edge_weight", "L0_gnn_W_edge", "L0_gnn_b_edge", "L0_gnn_W_self",
        "L0_gnn_b_self", "L0_gnn_attention"]


def kernel(**inputs):
    import numpy as np
    import concourse.bacc as bacc
    from concourse.bass_utils import run_bass_kernel_spmd

    nc = bacc.Bacc("TRN2", target_bir_lowering=False, num_devices=1)
    arrays, args = {}, []
    for name in _INS:
        a = np.ascontiguousarray(inputs[name])
        arrays[f"in_{name}_dram"] = a
        args.append(nc.dram_tensor(f"in_{name}_dram", a.shape, mybir.dt.from_np(a.dtype), kind="ExternalInput").ap())
    shape = arrays["in_x_dram"].shape
    args.append(nc.dram_tensor("out_dram", shape, mybir.dt.float32, kind="ExternalOutput").ap())
    gnn_layer(nc, *args)
    r = run_bass_kernel_spmd(nc, [arrays], core_ids=[0])
    return r.results[0]["out_dram"]
```

```python
import concourse.bass as bass
from concourse import mybir
from contextlib import ExitStack


def gnn_layer(nc, x, src, dst, edge_type, edge_weight, w_edge, b_edge, w_self, b_self, attention, out):
    fp32 = mybir.dt.float32
    i32 = mybir.dt.int32
    ALU = mybir.AluOpType
    ACT = mybir.ActivationFunctionType
    AX = mybir.AxisListType
    ds = bass.ds

    P = 128
    NODES, D = x.shape
    EDGES = src.shape[0]
    TYPES = w_edge.shape[0]
    TPG = 4
    GE = TPG * P
    GROUPS = -(-EDGES // GE)
    LAST_EDGES = EDGES - (GROUPS - 1) * GE
    LAST_TILES = -(-LAST_EDGES // P)
    RING = 3
    ITERS = (GROUPS - 1) // RING
    assert ITERS * RING == GROUPS - 1
    WIN = 42
    SW = TYPES * WIN
    BLOCKS = -(-NODES // P)
    LAST_ROWS = NODES - (BLOCKS - 1) * P
    COLS = BLOCKS * P
    assert NODES + WIN <= COLS and BLOCKS < ITERS
    EPS = 1e-5
    ROWC = -(-GROUPS // P)
    ROWS = [min(P, GROUPS - c * P) for c in range(ROWC)]
    PREP = 3
    PIECES = PREP * RING
    assert (1 + (ROWC - 1) * PREP) * RING < P and ROWC * P >= GROUPS
    SELF = TPG
    OUTB = 7
    OSTEPS = BLOCKS // OUTB
    assert OSTEPS * OUTB == BLOCKS and OSTEPS % 2 == 0
    PACE = 2
    EARLY_ITER = BLOCKS + 1
    EARLY = OSTEPS - 2
    EARLY_END = EARLY_ITER + PACE * EARLY
    EARLY_G = (EARLY_ITER - 1) * RING
    assert EARLY % 2 == 0 and EARLY_END < ITERS - 1
    ZC = COLS // 16
    SPLIT = 4

    ctx = ExitStack()
    with ctx:
        def sb(name, shape, dt=fp32):
            return ctx.enter_context(nc.sbuf_tensor(name, shape, dt))

        def sem(name):
            return ctx.enter_context(nc.semaphore(name))

        acc = sb("acc", [P, COLS])
        xres = sb("xres", [P, BLOCKS * D])
        src_row = sb("src_row", [P, ROWC, GE], i32)
        dst_row = sb("dst_row", [P, ROWC, GE], i32)
        typ_row = sb("typ_row", [P, ROWC, GE], i32)
        ew_row = sb("ew_row", [P, ROWC, GE])
        srcf_row = sb("srcf_row", [P, GE])
        rel_row = sb("rel_row", [P, GE])
        side_row = sb("side_row", [P, GE])
        typ1_row = sb("typ1_row", [P, GE])
        key_row = sb("key_row", [P, GE])
        first_dst = sb("first_dst", [P, 4])
        base_col = sb("base_col", [P, 2])
        shift = sb("shift", [P, 1])
        src_all = sb("src_all", [P, GROUPS * TPG])
        meta_all = sb("meta_all", [P, GROUPS * 2 * TPG])
        base_row = sb("base_row", [1, GROUPS], i32)
        span_row = sb("span_row", [1, GROUPS])
        span_max = sb("span_max", [1, 1], i32)
        need_row = sb("need_row", [1, GROUPS - EARLY_G], i32)
        slack_row = sb("slack_row", [1, GROUPS - EARLY_G])
        slack = sb("slack", [1, 2])
        early_cell = sb("early_cell", [1, 1], i32)
        idx = sb("idx", [P, RING, TPG], i32)
        meta = sb("meta", [P, RING, 2 * TPG])
        raw = sb("raw", [P, RING, TPG * D])
        stats = sb("stats", [P, RING, TPG + 1, 6])
        meanvar = sb("meanvar", [P, RING, TPG + 1, 2])
        negmean = sb("negmean", [P, RING, TPG + 1])
        std = sb("std", [P, RING, TPG + 1])
        rstd = sb("rstd", [P, RING, TPG + 1])
        scale = sb("scale", [P, RING, TPG])
        hid = sb("hid", [P, RING, TPG, D])
        select = sb("select", [P, RING, TPG, SW])
        sums = sb("sums", [P, 2, TYPES, RING, WIN])
        hid_self = sb("hid_self", [P, D])
        diag = sb("diag", [P, P])
        hidT_self = sb("hidT_self", [P, P])
        gel = sb("gel", [P, 2, OUTB * P])
        ident = sb("ident", [P, P])
        iota_i = sb("iota_i", [P, SW], i32)
        iota = sb("iota", [P, SW])
        zeros = sb("zeros", [P, ZC])
        eps = sb("eps", [P, 1])
        gelu_zero = sb("gelu_zero", [P, 1])
        wts = sb("wts", [P, TYPES, D])
        wself = sb("wself", [P, D])
        bias = sb("bias", [P, TYPES, D])
        bself = sb("bself", [P, 1])
        att = sb("att", [P, TYPES + 1])
        att_max = sb("att_max", [P, 2])
        att_sum = sb("att_sum", [P, 2])

        def bank(name):
            return ctx.enter_context(nc.psum_tensor(name, [P, 512], fp32))

        agg = [bank(f"agg{i}") for i in range(RING)]
        through = bank("through")
        selfT = bank("selfT")
        selfO = bank("selfO")
        prepA = bank("prepA")
        prepB = bank("prepB")
        outA, outB = [prepA, prepB], [selfT, selfO]

        consts_ready = sem("consts_ready")
        pool_step = sem("pool_step")
        att_loaded = sem("att_loaded")
        wts_loaded = sem("wts_loaded")
        acc_zeroed = sem("acc_zeroed")
        x_loaded = sem("x_loaded")
        prep_step = sem("prep_step")
        exp_done = sem("exp_done")
        max_done = sem("max_done")
        bias_zeroed = sem("bias_zeroed")
        settled = sem("settled")
        weights_ready = sem("weights_ready")
        early_step = sem("early_step")
        span_ready = sem("span_ready")
        src_loaded = [sem(f"src_loaded{c}") for c in range(ROWC)]
        row_loaded = [sem(f"row_loaded{c}") for c in range(ROWC)]
        srcf_ready = sem("srcf_ready")
        srcT_done = sem("srcT_done")
        srcT_copied = sem("srcT_copied")
        ewT_done = sem("ewT_done")
        ewT_copied = sem("ewT_copied")
        base_ready = sem("base_ready")
        baseT_done = sem("baseT_done")
        baseT_copied = sem("baseT_copied")
        row_step = sem("row_step")
        key_ready = sem("key_ready")
        keyT_done = sem("keyT_done")
        keyT_copied = sem("keyT_copied")
        slot_free = sem("slot_free")
        gathered = [sem(f"gathered{u}") for u in range(RING)]
        meta_ready = sem("meta_ready")
        bn_done = sem("bn_done")
        aggr_done = sem("aggr_done")
        stats_ready = sem("stats_ready")
        std_ready = sem("std_ready")
        rstd_done = sem("rstd_done")
        scale_done = sem("scale_done")
        hid_ready = sem("hid_ready")
        select_ready = sem("select_ready")
        summed = sem("summed")
        sums_ready = sem("sums_ready")
        acc_added = sem("acc_added")
        weighted = sem("weighted")
        selfT_done = sem("selfT_done")
        selfT_ready = sem("selfT_ready")
        self_done = sem("self_done")
        self_added = sem("self_added")
        gel_ready = sem("gel_ready")
        gelT_done = sem("gelT_done")
        out_ready = sem("out_ready")
        out_stored = sem("out_stored")

        SRC_DMAS = [1] * (ROWC - 1) + [3]
        ROW_DMAS = [3] * (ROWC - 1) + [8]
        GATHER_INC = [16 * TPG * ITERS + (16 * LAST_TILES if u == 0 else 0) for u in range(RING)]

        def settle(eng):
            eng.sem_inc(settled, 1)

        def tiles(g):
            return LAST_TILES if isinstance(g, int) and g == GROUPS - 1 else TPG

        def there(g):
            return not isinstance(g, int) or 0 <= g < GROUPS

        def late(g):
            return not isinstance(g, int) or g >= RING

        def load_early(eng, p, early):
            eng.wait_ge(span_ready, p + 1)
            settle(eng)
            eng.load(early, early_cell[0:1, 0:1])

        def chosen(eng, early, value):
            is_early = eng.snap(early, min_val=0, max_val=1)
            settle(eng)
            return eng.If(is_early > 0) if value else eng.If(is_early < 1)

        def walk(eng, p, step, piece, output=None, early=None):
            for c in range(ROWC):
                if c == 0:
                    for i in range(PIECES):
                        piece(i, c)
                    for u in range(RING):
                        step(0, u, u, True)
                    continue
                for i in range(PIECES):
                    g = RING + (c - 1) * PIECES + i
                    step(g // RING, g % RING, g, True)
                    piece(i, c)
            with eng.Fori(1 + (ROWC - 1) * PREP, BLOCKS) as it:
                g0 = eng.snap(it * RING)
                for u in range(RING):
                    step(it, u, g0 + u, True)
            if output:
                load_early(eng, p, early)
            for g in range(BLOCKS * RING, (BLOCKS + 1) * RING):
                step(g // RING, g % RING, g, False)

            def iterations(lo, hi):
                with eng.Fori(lo, hi) as it:
                    g0 = eng.snap(it * RING)
                    for u in range(RING):
                        step(it, u, g0 + u, False)

            if output:
                with chosen(eng, early, 1):
                    with eng.Fori(0, EARLY - 1, 2) as o:
                        for k in range(2):
                            for i in range(PACE):
                                it = eng.snap(o * PACE + (EARLY_ITER + k * PACE + i))
                                g0 = eng.snap(it * RING)
                                for u in range(RING):
                                    step(it, u, g0 + u, False)
                                    output(it, i * RING + u, o + k, k)
                with chosen(eng, early, 0):
                    iterations(EARLY_ITER, EARLY_END)
                iterations(EARLY_END, ITERS - 1)
            else:
                iterations(EARLY_ITER, ITERS - 1)
            for g in range((ITERS - 1) * RING, (ITERS + 2) * RING + 1):
                step(g // RING, g % RING, g, False)

        def passes(eng, body, end=None):
            limit = eng.alloc_register("pass_limit")
            eng.reg_mov(limit, 1)
            with eng.Fori(0, limit) as p:
                body(p)
                eng.wait_ge(span_ready, p + 1)
                settle(eng)
                eng.load(limit, span_max[0:1, 0:1])
                eng.reg_div(limit, limit, WIN)
                eng.reg_add(limit, limit, 1)
                if end:
                    end(p)

        block = ctx.enter_context(nc.Block())

        @block.sync
        def _(sp):
            def one_pass(p):
                for c in range(ROWC - 1):
                    lo, hi = c * P * GE, (c + 1) * P * GE
                    if c > 0:
                        sp.wait_ge(gathered[c - 1], p * GATHER_INC[c - 1] + 16 * TPG)
                    sp.dma_start(src_row[:, c, :], src[lo:hi].rearrange("(p e) -> p e", p=P)).then_inc(src_loaded[c], 16)
                    sp.dma_start(dst_row[:, c, :], dst[lo:hi].rearrange("(p e) -> p e", p=P)).then_inc(row_loaded[c], 16)
                    sp.dma_start(typ_row[:, c, :], edge_type[lo:hi].rearrange("(p e) -> p e", p=P)).then_inc(row_loaded[c], 16)
                    sp.dma_start(ew_row[:, c, :], edge_weight[lo:hi].rearrange("(p e) -> p e", p=P)).then_inc(row_loaded[c], 16)
                    if c == 0:
                        with sp.If(p < 1):
                            sp.dma_start(xres[:, 0:D], x[0:P, :]).then_inc(x_loaded, 16)
                            sp.dma_start(wts[:, :, :], w_edge.rearrange("t i o -> i t o")).then_inc(wts_loaded, 16)
                            sp.dma_start(wself[:, :], w_self[:, :]).then_inc(wts_loaded, 16)
                            sp.dma_start(bself[:, :], b_self.unsqueeze(1)).then_inc(wts_loaded, 16)
                            sp.wait_ge(bias_zeroed, 1)
                            sp.dma_start(bias[0:1, :, :], b_edge.unsqueeze(0)).then_inc(wts_loaded, 16)
                c, n = ROWC - 1, ROWS[-1] - 1
                lo, hi = c * P * GE, (GROUPS - 1) * GE
                fill = GE - LAST_EDGES
                sp.wait_ge(consts_ready, 1)
                for a, rows, signal in ((src, src_row, src_loaded[c]), (dst, dst_row, row_loaded[c]),
                                        (edge_type, typ_row, row_loaded[c]), (edge_weight, ew_row, row_loaded[c])):
                    sp.dma_start(rows[0:n, c, :], a[lo:hi].rearrange("(p e) -> p e", p=n)).then_inc(signal, 16)
                    sp.dma_start(rows[n:n + 1, c, 0:LAST_EDGES], a[hi:EDGES].rearrange("(p e) -> p e", p=1)).then_inc(signal, 16)
                    if a is not edge_weight:
                        sp.dma_start(rows[n:n + 1, c, LAST_EDGES:GE], a[EDGES - fill:EDGES].rearrange("(p e) -> p e", p=1)).then_inc(signal, 16)
                with sp.If(p < 1):
                    with sp.Fori(1, BLOCKS - 1) as b:
                        sp.wait_ge(x_loaded, b * 16)
                        sp.dma_start(xres[:, ds(b * D, D)], x[ds(b * P, P), :]).then_inc(x_loaded, 16)
                    sp.wait_ge(x_loaded, (BLOCKS - 1) * 16)
                    sp.dma_start(xres[0:LAST_ROWS, (BLOCKS - 1) * D:], x[(BLOCKS - 1) * P:, :]).then_inc(x_loaded, 16)
                load_early(sp, p, early)
                with chosen(sp, early, 1):
                    stores(0, EARLY)
                sp.wait_ge(acc_added, (p + 1) * GROUPS)

            def stores(lo, hi):
                with sp.Fori(lo, hi) as o:
                    sp.wait_ge(out_ready, 2 + o + 1)
                    sp.dma_start(out[ds(o * (OUTB * P), OUTB * P), :].rearrange("(b p) d -> p b d", p=P),
                                 xres[:, ds(o * (OUTB * D), OUTB * D)].rearrange("p (b d) -> p b d", d=D)).then_inc(out_stored, 16)

            early = sp.alloc_register("early")
            passes(sp, one_pass)
            with chosen(sp, early, 0):
                stores(0, EARLY)
            stores(EARLY, OSTEPS - 1)
            sp.wait_ge(out_ready, 2 + OSTEPS)
            b0 = (OSTEPS - 1) * OUTB
            sp.dma_start(out[b0 * P:(BLOCKS - 1) * P, :].rearrange("(b p) d -> p b d", p=P),
                         xres[:, b0 * D:(BLOCKS - 1) * D].rearrange("p (b d) -> p b d", d=D)).then_inc(out_stored, 16)
            sp.dma_start(out[(BLOCKS - 1) * P:, :], xres[0:LAST_ROWS, (BLOCKS - 1) * D:]).then_inc(out_stored, 16)
            sp.wait_ge(out_stored, 16 * (OSTEPS + 1))

        @block.gpsimd
        def _(pool):
            nc.gpsimd.memset(ew_row[:, ROWC - 1, :], 0.0)
            nc.gpsimd.memset(xres[:, (BLOCKS - 1) * D:], 0.0)
            nc.gpsimd.memset(zeros[:, :], 0.0)
            nc.gpsimd.memset(eps[:, :], EPS)
            nc.gpsimd.memset(shift[:, :], 0.0)
            nc.gpsimd.iota(iota_i[:, :], pattern=[[1, SW]], base=1, channel_multiplier=0)
            nc.gpsimd.memset(ident[:, :], 0.0).then_inc(pool_step, 1)
            pool.wait_ge(pool_step, 1)
            nc.gpsimd.affine_select(out=ident[:, :], in_=ident[:, :], compare_op=ALU.not_equal, fill=1.0,
                                    base=0, pattern=[[-1, P]], channel_multiplier=1)
            nc.gpsimd.tensor_copy(iota[:, :], iota_i[:, :])
            stairs = EARLY * PACE * RING
            nc.gpsimd.iota(need_row[:, 0:stairs], pattern=[[OUTB * P, EARLY], [0, PACE * RING]], base=OUTB * P, channel_multiplier=0)
            nc.gpsimd.iota(need_row[:, stairs:], pattern=[[0, GROUPS - EARLY_G - stairs]], base=EARLY * OUTB * P, channel_multiplier=0)
            nc.gpsimd.drain().then_inc(consts_ready, 1)
            nc.gpsimd.memset(acc[:, 0:3 * ZC], 0.0).then_inc(acc_zeroed, 1)

            def one_pass(p):
                def step(it, u, g, with_block):
                    if not there(g):
                        return
                    pool.wait_ge(slot_free, p * GROUPS + g + 1)
                    settle(pool)
                    for j in range(tiles(g)):
                        nc.gpsimd.indirect_dma_start(
                            raw[:, u, j * D:(j + 1) * D], None, x[:, :],
                            bass.IndirectOffsetOnAxis(ap=idx[:, u, j:j + 1], axis=0)).then_inc(gathered[u], 16)

                walk(pool, p, step, lambda i, c: None)

            passes(pool, one_pass)

        @block.scalar
        def _(act):
            act.dma_start(att[:, :], attention.unsqueeze(0).to_broadcast([P, TYPES + 1])).then_inc(att_loaded, 16)

            def one_pass(p):
                def piece(i, c):
                    R = ROWS[c]
                    C = p * ROWC + c
                    groups = slice(c * P, c * P + R)
                    if i == 0:
                        act.wait_ge(src_loaded[c], (p + 1) * (16 * SRC_DMAS[c]))
                        if c > 0:
                            act.wait_ge(srcT_done, C)
                        nc.scalar.copy(srcf_row[0:R, :], src_row[0:R, c, :]).then_inc(srcf_ready, 1)
                    if i == 3:
                        act.wait_ge(srcT_done, C + 1)
                        nc.scalar.copy(src_all[:, c * P * TPG:(c * P + R) * TPG].rearrange("p (r j) -> p j r", j=TPG),
                                       prepA[:, 0:TPG * R].rearrange("p (j r) -> p j r", j=TPG)).then_inc(srcT_copied, 1)
                        act.wait_ge(srcT_copied, C + 1)
                        if c == 0:
                            for u in range(RING):
                                nc.scalar.copy(idx[:, u, :], src_all[:, u * TPG:(u + 1) * TPG]).then_inc(slot_free, 1)
                            with act.If(p < 1):
                                act.wait_ge(max_done, 2)
                                nc.scalar.activation(att[:, :], att[:, :], ACT.Exp, bias=att_max[:, 1:2],
                                                     accum_out=att_sum[:, 0:1]).then_inc(exp_done, 1)
                                act.wait_ge(consts_ready, 1)
                                half = COLS // 2
                                nc.scalar.copy(acc[:, half:].rearrange("p (r c) -> p r c", r=half // ZC),
                                               zeros[:, :].unsqueeze(1).to_broadcast([P, half // ZC, ZC])).then_inc(acc_zeroed, 1)
                    if i == 5:
                        act.wait_ge(ewT_done, C + 1)
                        nc.scalar.copy(meta_all[:, c * P * 2 * TPG:(c * P + R) * 2 * TPG].rearrange(
                            "p (r s j) -> p s j r", s=2, j=TPG)[:, 1],
                                       prepA[:, 0:TPG * R].rearrange("p (j r) -> p j r", j=TPG)).then_inc(ewT_copied, 1)
                    if i == PIECES - 1:
                        act.wait_ge(ewT_copied, C + 1)
                        act.wait_ge(keyT_copied, C + 1)

                def step(it, u, g, with_block):
                    G = p * GROUPS + g
                    B = p * BLOCKS + it
                    n = tiles(g)
                    if there(g):
                        if late(g):
                            act.wait_ge(select_ready, G - (RING - 1))
                        nc.scalar.copy(meta[:, u, :], meta_all[:, ds(g * (2 * TPG), 2 * TPG)]).then_inc(meta_ready, 1)
                        act.wait_ge(stats_ready, G + 1)
                        if late(g):
                            act.wait_ge(summed, G - (RING - 1))
                        m = n + 1 if with_block and u == 0 else n
                        nc.scalar.activation(std[:, u, 0:m], meanvar[:, u, 0:m, 1], ACT.Sqrt,
                                             bias=eps[:, 0:1]).then_inc(std_ready, 1)
                        if with_block and u == 0:
                            if not isinstance(it, int) or it > 0:
                                act.wait_ge(selfT_done, B)
                            nc.scalar.activation(hid_self[:, :], xres[:, ds(it * D, D)], ACT.Relu,
                                                 bias=negmean[:, u, SELF:SELF + 1])
                        for j in range(n):
                            last = nc.scalar.activation(hid[:, u, j, :], raw[:, u, j * D:(j + 1) * D], ACT.Relu,
                                                        bias=negmean[:, u, j:j + 1])
                        last.then_inc(hid_ready, 1)
                        if not isinstance(g, int) or g + RING < GROUPS:
                            act.wait_ge(hid_ready, G + 1)
                            nc.scalar.copy(idx[:, u, :], src_all[:, ds((g + RING) * TPG, TPG)]).then_inc(slot_free, 1)
                    if with_block and u == RING - 1:
                        act.wait_ge(selfT_done, B + 1)
                        if not isinstance(it, int) or it > 0:
                            act.wait_ge(self_done, B)
                        nc.scalar.copy(hidT_self[:, :], selfT[:, 0:P]).then_inc(selfT_ready, 1)
                    k, v = g - 2, (u - 2) % RING
                    if there(k):
                        act.wait_ge(summed, G - 1)
                        if v == 0 and (not isinstance(k, int) or k > 0):
                            act.wait_ge(weighted, p * (ITERS + 1) + it)
                        nc.scalar.copy(sums[:, :, :, v, :], agg[v][:, 0:2 * SW].rearrange(
                            "p (s t w) -> p s t w", s=2, t=TYPES)).then_inc(sums_ready, 1)

                def output(it, u, o, k):
                    if u == 1:
                        act.wait_ge(acc_added, p * GROUPS + (it - 1) * RING)
                        act.wait_ge(self_added, (p + 1) * BLOCKS)
                        out_step(o, k)

                walk(act, p, step, piece, output, early)
            def out_step(o, k):
                act.wait_ge(gelT_done, o + 1)
                nc.scalar.activation(gel[:, k, :], acc[:, ds(o * (OUTB * P), OUTB * P)], ACT.Gelu).then_inc(gel_ready, 1)

            early = act.alloc_register("early")
            def end(p):
                nc.scalar.activation(gelu_zero[:, :], zeros[:, 0:1], ACT.Gelu)
                act.wait_ge(acc_added, (p + 1) * GROUPS)

            passes(act, one_pass, end)
            with chosen(act, early, 0):
                with act.Fori(0, EARLY - 1, 2) as o:
                    out_step(o, 0)
                    out_step(o + 1, 1)
            for o in range(EARLY, OSTEPS):
                out_step(o, o % 2)

        @block.vector
        def _(dve):
            nc.vector.memset(bias[:, :, :], 0.0).then_inc(bias_zeroed, 1)
            nc.vector.memset(acc[:, 3 * ZC:5 * ZC], 0.0)
            dve.wait_ge(att_loaded, 16)
            nc.vector.tensor_reduce(out=att_max[:, 0:1], in_=att[:, :], axis=AX.X, op=ALU.max).then_inc(max_done, 1)
            dve.wait_ge(max_done, 1)
            nc.vector.tensor_scalar(att_max[:, 1:2], att_max[:, 0:1], -1.0, None, ALU.mult).then_inc(max_done, 1)
            nc.vector.memset(acc[:, 5 * ZC:8 * ZC], 0.0).then_inc(acc_zeroed, 1)
            dve.wait_ge(consts_ready, 1)

            def weights():
                dve.wait_ge(exp_done, 1)
                nc.vector.reciprocal(att_sum[:, 1:2], att_sum[:, 0:1]).then_inc(prep_step, 1)
                dve.wait_ge(prep_step, 1)
                nc.vector.tensor_scalar(att[:, :], att[:, :], att_sum[:, 1:2], None, ALU.mult).then_inc(prep_step, 1)
                dve.wait_ge(prep_step, 2)
                dve.wait_ge(wts_loaded, 16 * 4)
                for t in range(TYPES):
                    nc.vector.tensor_scalar(wts[:, t, :], wts[:, t, :], att[:, t:t + 1], None, ALU.mult)
                    nc.vector.tensor_scalar(bias[:, t, :], bias[:, t, :], att[:, t:t + 1], None, ALU.mult)
                nc.vector.tensor_scalar(wself[:, :], wself[:, :], att[:, TYPES:TYPES + 1], None, ALU.mult)
                nc.vector.tensor_scalar(bself[:, :], bself[:, :], att[:, TYPES:TYPES + 1], None, ALU.mult).then_inc(weights_ready, 1)

            ORDER = 4

            base_regs = [dve.alloc_register(f"base{v}") for v in range(RING)]

            def one_pass(p):
                def piece(i, c):
                    R = ROWS[c]
                    C = p * ROWC + c
                    S = C * ORDER
                    d = dst_row[0:R, c, :]
                    if i == 0:
                        dve.wait_ge(row_loaded[c], (p + 1) * (16 * ROW_DMAS[c]))
                        nc.vector.tensor_reduce(out=first_dst[0:R, 0:1], in_=d, axis=AX.X, op=ALU.min)
                        nc.vector.tensor_reduce(out=first_dst[0:R, 1:2], in_=d, axis=AX.X, op=ALU.max).then_inc(row_step, 1)
                    if i == 1:
                        dve.wait_ge(row_step, S + 1)
                        if c > 0:
                            dve.wait_ge(baseT_done, C)
                        nc.vector.tensor_scalar(base_col[0:R, 0:1], first_dst[0:R, 0:1], shift[0:R, 0:1], float(NODES), ALU.add, ALU.min)
                        nc.vector.tensor_tensor(base_col[0:R, 1:2], first_dst[0:R, 1:2], first_dst[0:R, 0:1], ALU.subtract).then_inc(base_ready, 1)
                        dve.wait_ge(base_ready, C + 1)
                        nc.vector.tensor_scalar(first_dst[0:R, 2:3], base_col[0:R, 0:1], -1.0, None, ALU.add)
                        nc.vector.tensor_scalar(first_dst[0:R, 3:4], base_col[0:R, 0:1], float(WIN), None, ALU.add).then_inc(row_step, 1)
                        dve.wait_ge(row_step, S + 2)
                        nc.vector.tensor_scalar(rel_row[0:R, :], d, first_dst[0:R, 2:3], None, ALU.subtract).then_inc(row_step, 1)
                    if i == 2:
                        dve.wait_ge(row_step, S + 3)
                        nc.vector.scalar_tensor_tensor(side_row[0:R, :], d, first_dst[0:R, 3:4], rel_row[0:R, :], ALU.subtract, ALU.mult)
                        nc.vector.scalar_tensor_tensor(typ1_row[0:R, :], typ_row[0:R, c, :], float(WIN), rel_row[0:R, :], ALU.mult, ALU.add).then_inc(row_step, 1)
                    if i == 3:
                        dve.wait_ge(row_step, S + 4)
                        if c > 0:
                            dve.wait_ge(keyT_done, C)
                        nc.vector.scalar_tensor_tensor(key_row[0:R, :], side_row[0:R, :], 0.0, typ1_row[0:R, :], ALU.is_lt, ALU.mult).then_inc(key_ready, 1)
                    if i == 4:
                        dve.wait_ge(baseT_done, C + 1)
                        nc.vector.tensor_copy(base_row[0:1, c * P:c * P + R], prepB[0:1, 0:R])
                        nc.vector.tensor_copy(span_row[0:1, c * P:c * P + R], prepB[0:1, P:P + R]).then_inc(baseT_copied, 1)
                    if i == 6:
                        dve.wait_ge(keyT_done, C + 1)
                        m = meta_all[:, c * P * 2 * TPG:(c * P + R) * 2 * TPG].rearrange("p (r s j) -> p s j r", s=2, j=TPG)
                        nc.vector.tensor_copy(m[:, 0], prepB[:, 0:TPG * R].rearrange("p (j r) -> p j r", j=TPG)).then_inc(keyT_copied, 1)
                    if i == PIECES - 1:
                        dve.wait_ge(baseT_copied, C + 1)
                        if c == ROWC - 1:
                            nc.vector.tensor_reduce(out=span_max[0:1, 0:1], in_=span_row[0:1, :], axis=AX.X, op=ALU.max)
                            nc.vector.tensor_tensor(slack_row[0:1, :], base_row[0:1, EARLY_G:], need_row[0:1, :], ALU.subtract).then_inc(early_step, 1)
                            dve.wait_ge(early_step, p * 3 + 1)
                            nc.vector.tensor_reduce(out=slack[0:1, 0:1], in_=slack_row[0:1, :], axis=AX.X, op=ALU.min).then_inc(early_step, 1)
                            dve.wait_ge(early_step, p * 3 + 2)
                            nc.vector.tensor_scalar(slack[0:1, 1:2], slack[0:1, 0:1], 0.0, None, ALU.is_ge).then_inc(early_step, 1)
                            dve.wait_ge(early_step, p * 3 + 3)
                            nc.vector.scalar_tensor_tensor(early_cell[0:1, 0:1], span_max[0:1, 0:1], float(WIN), slack[0:1, 1:2],
                                                           ALU.is_lt, ALU.mult).then_inc(span_ready, 1)

                def step(it, u, g, with_block):
                    G = p * GROUPS + g
                    B = p * BLOCKS + it
                    if there(g):
                        n = tiles(g)
                        m = n
                        if late(g):
                            dve.wait_ge(hid_ready, G - (RING - 1))
                        if with_block and u == 0:
                            m = n + 1
                            dve.wait_ge(x_loaded, it * 16 + 16)
                            nc.vector.bn_stats(out=stats[:, u, SELF, :], in_=xres[:, ds(it * D, D)])
                        dve.wait_ge(gathered[u], p * GATHER_INC[u] + (it * (16 * TPG) + 16 * n))
                        for j in range(n):
                            last = nc.vector.bn_stats(out=stats[:, u, j, :], in_=raw[:, u, j * D:(j + 1) * D])
                        last.then_inc(bn_done, 1)
                        dve.wait_ge(bn_done, G + 1)
                        settle(dve)
                        for j in range(m):
                            last = nc.vector.bn_aggr(out=meanvar[:, u, j, :], in_=stats[:, u, j, :])
                        last.then_inc(aggr_done, 1)
                        dve.wait_ge(aggr_done, G + 1)
                        nc.vector.tensor_scalar(negmean[:, u, 0:m], meanvar[:, u, 0:m, 0], -1.0, None, ALU.mult).then_inc(stats_ready, 1)
                    k, v = g - 1, (u - 1) % RING
                    if there(k):
                        n = tiles(k)
                        m = n + 1 if with_block and v == 0 else n
                        dve.wait_ge(std_ready, G)
                        nc.vector.reciprocal(rstd[:, v, 0:m], std[:, v, 0:m]).then_inc(rstd_done, 1)
                        dve.wait_ge(rstd_done, G)
                        dve.wait_ge(meta_ready, G)
                        nc.vector.tensor_tensor(scale[:, v, 0:n], meta[:, v, TPG:TPG + n], rstd[:, v, 0:n], ALU.mult).then_inc(scale_done, 1)
                        if m > n:
                            if not isinstance(it, int) or it > 0:
                                dve.wait_ge(selfT_done, B)
                            nc.vector.tensor_scalar(diag[:, :], ident[:, :], rstd[:, v, SELF:SELF + 1], None, ALU.mult)
                        dve.wait_ge(scale_done, G)
                        if late(k):
                            dve.wait_ge(summed, G - 1 - (RING - 1))
                        for j in range(n):
                            last = nc.vector.tensor_scalar(select[:, v, j, :], iota[:, :], meta[:, v, j:j + 1],
                                                           scale[:, v, j:j + 1], ALU.is_equal, ALU.mult)
                        last.then_inc(select_ready, 1)
                    if u == 2 and isinstance(it, int) and it == 0:
                        settle(dve)
                        with dve.If(p < 1):
                            weights()
                        dve.wait_ge(weights_ready, p + 1)
                    if u == RING - 1 and (not isinstance(it, int) or 0 < it <= ITERS + 1):
                        groups = RING if not isinstance(it, int) or it <= ITERS else GROUPS - ITERS * RING
                        dve.load(base_regs[0:groups], base_row[0:1, ds((it - 1) * RING, groups)])
                    if u == 0 and (not isinstance(it, int) or 1 < it <= ITERS + 2):
                        groups = RING if not isinstance(it, int) or it < ITERS + 2 else GROUPS - ITERS * RING
                        dve.wait_ge(weighted, p * (ITERS + 1) + (it - 1))
                        if with_block or isinstance(it, int) and it - 2 < BLOCKS:
                            dve.wait_ge(self_added, B - 1)
                        for v in range(groups):
                            if v > 0 or not isinstance(it, int) or it > 2:
                                dve.wait_ge(acc_added, p * GROUPS + ((it - 2) * RING + v))
                            base = dve.snap(base_regs[v], min_val=0, max_val=NODES)
                            nc.vector.tensor_tensor(acc[:, ds(base, WIN)], acc[:, ds(base, WIN)],
                                                    through[:, v * WIN:(v + 1) * WIN], ALU.add).then_inc(acc_added, 1)
                    if u == 1 and (with_block and not (isinstance(it, int) and it == 0) or isinstance(it, int) and it == BLOCKS):
                        dve.wait_ge(self_done, B)
                        if isinstance(it, int) and it == 1:
                            dve.wait_ge(acc_zeroed, 3)
                        else:
                            dve.wait_ge(acc_added, p * GROUPS + (it - 1) * RING)
                        nc.vector.scalar_tensor_tensor(acc[:, ds((it - 1) * P, P)], selfO[:, 0:P], bself[:, 0:1],
                                                       acc[:, ds((it - 1) * P, P)], ALU.add, ALU.add).then_inc(self_added, 1)

                def output(it, u, o, k):
                    if u == RING:
                        out_step(o, k)

                walk(dve, p, step, piece, output, early)
                dve.wait_ge(acc_added, (p + 1) * GROUPS)
                nc.vector.tensor_scalar(shift[:, :], shift[:, :], float(WIN), None, ALU.add)
                nc.vector.memset(wself[:, :], 0.0)
                nc.vector.memset(bself[:, :], 0.0).then_inc(weights_ready, 1)
                dve.wait_ge(weights_ready, p + 2)

            def out_step(o, k):
                dve.wait_ge(gelT_done, 2 + o + 1)
                lo, n0, n1 = o * (OUTB * D), SPLIT * D, (OUTB - SPLIT) * D
                nc.vector.tensor_tensor(xres[:, ds(lo, n0)], xres[:, ds(lo, n0)], outA[k][:, 0:n0], ALU.add)
                nc.vector.tensor_tensor(xres[:, ds(lo + n0, n1)], xres[:, ds(lo + n0, n1)], outB[k][:, 0:n1], ALU.add).then_inc(out_ready, 1)

            dve.sem_inc(out_ready, 2)
            early = dve.alloc_register("early")
            passes(dve, one_pass)
            with chosen(dve, early, 0):
                with dve.Fori(0, EARLY - 1, 2) as o:
                    out_step(o, 0)
                    out_step(o + 1, 1)
            for o in range(EARLY, OSTEPS):
                out_step(o, o % 2)

        @block.tensor
        def _(pe):
            pe.wait_ge(consts_ready, 1)

            def one_pass(p):
                def piece(i, c):
                    R = ROWS[c]
                    C = p * ROWC + c
                    if i == 1:
                        pe.wait_ge(srcf_ready, C + 1)
                        if c > 0:
                            pe.wait_ge(ewT_copied, C)
                        settle(pe)
                        for j in range(TPG):
                            last = nc.tensor.transpose(prepA[:, j * R:(j + 1) * R], srcf_row[0:R, j * P:(j + 1) * P], ident[0:R, 0:R])
                        last.then_inc(srcT_done, 1)
                    if i == 2:
                        pe.wait_ge(base_ready, C + 1)
                        if c > 0:
                            pe.wait_ge(keyT_copied, C)
                        settle(pe)
                        nc.tensor.transpose(prepB[0:1, 0:R], base_col[0:R, 0:1], ident[0:R, 0:R])
                        nc.tensor.transpose(prepB[0:1, P:P + R], base_col[0:R, 1:2], ident[0:R, 0:R]).then_inc(baseT_done, 1)
                    if i == 3:
                        pe.wait_ge(row_loaded[c], (p + 1) * (16 * ROW_DMAS[c]))
                        pe.wait_ge(srcT_copied, C + 1)
                        settle(pe)
                        for j in range(TPG):
                            last = nc.tensor.transpose(prepA[:, j * R:(j + 1) * R], ew_row[0:R, c, j * P:(j + 1) * P], ident[0:R, 0:R])
                        last.then_inc(ewT_done, 1)
                    if i == 4:
                        pe.wait_ge(key_ready, C + 1)
                        pe.wait_ge(baseT_copied, C + 1)
                        settle(pe)
                        for j in range(TPG):
                            last = nc.tensor.transpose(prepB[:, j * R:(j + 1) * R], key_row[0:R, j * P:(j + 1) * P], ident[0:R, 0:R])
                        last.then_inc(keyT_done, 1)

                def step(it, u, g, with_block):
                    G = p * GROUPS + g
                    B = p * BLOCKS + it
                    if u == 1 and (not isinstance(it, int) or 0 < it <= ITERS + 1):
                        pe.wait_ge(weights_ready, p + 1)
                        done = p * GROUPS + (GROUPS if isinstance(it, int) and it == ITERS + 1 else it * RING)
                        pe.wait_ge(sums_ready, done)
                        if not isinstance(it, int) or it > 1:
                            pe.wait_ge(acc_added, p * GROUPS + (it - 1) * RING)
                        for t in range(TYPES):
                            nc.tensor.matmul(through[:, 0:SW], wts[:, t, :], sums[:, 0, t, :, :].rearrange("p u w -> p (u w)"),
                                             start=t == 0, stop=False)
                        for t in range(TYPES):
                            last = nc.tensor.matmul(through[:, 0:SW], bias[:, t, :], sums[:, 1, t, :, :].rearrange("p u w -> p (u w)"),
                                                    start=False, stop=t == TYPES - 1)
                        last.then_inc(weighted, 1)
                    if with_block and u == RING - 1:
                        pe.wait_ge(selfT_ready, B + 1)
                        if isinstance(it, int) and it == 0:
                            pe.wait_ge(weights_ready, p + 1)
                        if not isinstance(it, int) or it > 0:
                            pe.wait_ge(self_added, B)
                        nc.tensor.matmul(selfO[:, 0:P], wself[:, :], hidT_self[:, :], start=True, stop=True).then_inc(self_done, 1)
                    if there(g):
                        n = tiles(g)
                        pe.wait_ge(hid_ready, G + 1)
                        pe.wait_ge(select_ready, G + 1)
                        if late(g):
                            pe.wait_ge(sums_ready, G - (RING - 1))
                        for j in range(n):
                            nc.tensor.matmul(agg[u][:, 0:SW], hid[:, u, j, :], select[:, u, j, :], start=j == 0, stop=False)
                            last = nc.tensor.matmul(agg[u][:, SW:2 * SW], std[:, u, j:j + 1].to_broadcast([P, P]),
                                                    select[:, u, j, :], start=False, stop=j == n - 1)
                        last.then_inc(summed, 1)
                        if with_block and u == 0:
                            if not isinstance(it, int) or it > 0:
                                pe.wait_ge(selfT_ready, B)
                            nc.tensor.matmul(selfT[:, 0:P], hid_self[:, :], diag[:, :], start=True, stop=True).then_inc(selfT_done, 1)

                def output(it, u, o, k):
                    if u == 1:
                        out_step(o, k)

                walk(pe, p, step, piece, output, early)

            def out_step(o, k):
                pe.wait_ge(gel_ready, o + 1)
                pe.wait_ge(out_ready, o + 1)
                for b in range(OUTB):
                    to = outA[k][:, b * P:(b + 1) * P] if b < SPLIT else outB[k][:, (b - SPLIT) * P:(b - SPLIT + 1) * P]
                    last = nc.tensor.transpose(to, gel[:, k, b * P:(b + 1) * P], ident[:, :])
                last.then_inc(gelT_done, 1)

            pe.sem_inc(gelT_done, 2)
            early = pe.alloc_register("early")
            passes(pe, one_pass)
            with chosen(pe, early, 0):
                with pe.Fori(0, EARLY - 1, 2) as o:
                    out_step(o, 0)
                    out_step(o + 1, 1)
            for o in range(EARLY, OSTEPS):
                out_step(o, o % 2)


_INS = ["x", "src", "dst", "edge_type_3", "edge_weight", "L0_gnn_W_edge", "L0_gnn_b_edge", "L0_gnn_W_self",
        "L0_gnn_b_self", "L0_gnn_attention"]


def kernel(**inputs):
    import numpy as np
    import concourse.bacc as bacc
    from concourse.bass_utils import run_bass_kernel_spmd

    nc = bacc.Bacc("TRN2", target_bir_lowering=False, num_devices=1)
    arrays, args = {}, []
    for name in _INS:
        a = np.ascontiguousarray(inputs[name])
        arrays[f"in_{name}_dram"] = a
        args.append(nc.dram_tensor(f"in_{name}_dram", a.shape, mybir.dt.from_np(a.dtype), kind="ExternalInput").ap())
    shape = arrays["in_x_dram"].shape
    args.append(nc.dram_tensor("out_dram", shape, mybir.dt.float32, kind="ExternalOutput").ap())
    gnn_layer(nc, *args)
    r = run_bass_kernel_spmd(nc, [arrays], core_ids=[0])
    return r.results[0]["out_dram"]
```
